# Optimizing a Trainium2 kernel written in Bass

```python
import numpy as np
import jax
import jax.numpy as jnp

def _softmax(x, axis=-1):
    return jax.nn.softmax(x, axis=axis)

def _gelu(x):
    return jax.nn.gelu(x, approximate=True)

def _silu(x):
    return jax.nn.silu(x)

def _sigmoid(x):
    return jax.nn.sigmoid(x)

def _layernorm(x, axis=-1, eps=1e-05):
    m = jnp.mean(x, axis=axis, keepdims=True)
    v = jnp.var(x, axis=axis, keepdims=True)
    return (x - m) / jnp.sqrt(v + eps)

def _scatter_add(tgt, idx, src, axis=0):
    return tgt.at[idx].add(src)

def _segment_sum(src, seg, n):
    return jax.ops.segment_sum(src, seg, n)
kernel_name = 'mk_gnn_ffn_d2_gnn_r32_cc86c4'

def setup_inputs(seed: int=0):
    np.random.seed(seed)
    _w = jnp.asarray

    def _rec_inputs():
        import jax
        import jax.numpy as jnp
        _gk = jax.random.key(seed)
        x = -0.0002928 + 1 * jax.random.normal(jax.random.fold_in(_gk, 1), (256, 512), jnp.float32)
        _s = jax.random.randint(jax.random.fold_in(_gk, 2), (2048,), 0, 256, jnp.int32)
        _d = jax.random.randint(jax.random.fold_in(_gk, 3), (2048,), 0, 256, jnp.int32)
        _loop = jnp.arange(256, dtype=jnp.int32)
        src = jnp.concatenate([_s, _d, _loop])
        dst = jnp.concatenate([_d, _s, _loop])
        _o = jnp.argsort(dst, stable=True)
        src = src[_o]
        dst = dst[_o]
        edge_attr_512 = -8.16379e-05 + 0.999858 * jax.random.normal(jax.random.fold_in(_gk, 12), (4352, 512), jnp.float32)
        return (x, src, dst, edge_attr_512)
    x, src, dst, edge_attr_512 = _rec_inputs()

    def _L0_gnn_setup():
        import jax, jax.numpy as jnp
        import numpy as np
        N = 256
        D = 512
        E = 8192
        STEPS = 3
        key = jax.random.key(seed)
        k1, k2, k3 = jax.random.split(key, 3)
        x = jax.random.normal(k1, (N, D), dtype=jnp.float32)
        edge_index = jax.random.randint(k2, (2, E), 0, N, dtype=jnp.int32)
        W = jax.random.normal(k3, (D, D), dtype=jnp.float32) / np.sqrt(D)
        b = jnp.zeros((D,), dtype=jnp.float32)
        diffusion_weights = jnp.ones((STEPS + 1,), dtype=jnp.float32) / (STEPS + 1)
        return {'x': x, 'edge_index': edge_index, 'W': W, 'b': b, 'diffusion_weights': diffusion_weights}
    _L0_gnn_all = _L0_gnn_setup()
    _L0_gnn_in = {k: v for k, v in _L0_gnn_all.items() if k in ('W', 'b', 'diffusion_weights')}
    del _L0_gnn_all

    def _L0_ffn_setup():
        import jax, jax.numpy as jnp
        import numpy as np
        G = 4
        EPG = 4
        E = 16
        KG = 2
        K = 2
        GTP = 0.9
        TP = 0.9
        SCALE = 1.0 / float(np.sqrt(G))

        def _routing_weights(xf, Wr, br, Wgate, bgate):
            N = xf.shape[0]
            gp = jax.nn.softmax(xf @ Wr + br, axis=-1)
            order = jnp.argsort(-gp, axis=-1)
            sp_k = jnp.take_along_axis(gp, order, axis=-1)[:, :KG]
            idx_k = order[:, :KG]
            act = jnp.cumsum(sp_k, axis=-1) <= GTP
            act = act.at[:, 0].set(True)
            mp = sp_k * act
            rn = mp / (jnp.sum(mp, axis=-1, keepdims=True) + 1e-09)
            w_group = jnp.zeros((N, G), xf.dtype).at[jnp.arange(N)[:, None], idx_k].set(rn)
            ep = jax.nn.softmax(jnp.einsum('nd,gde->nge', xf, Wgate) + bgate, axis=-1)
            eorder = jnp.argsort(-ep, axis=-1)
            esp = jnp.take_along_axis(ep, eorder, axis=-1)[:, :, :K]
            eidx = eorder[:, :, :K]
            eact = jnp.cumsum(esp, axis=-1) <= TP
            eact = eact.at[:, :, 0].set(True)
            emp = esp * eact
            ern = emp / (jnp.sum(emp, axis=-1, keepdims=True) + 1e-09)
            w_exp = jnp.zeros((N, G, EPG), xf.dtype).at[jnp.arange(N)[:, None, None], jnp.arange(G)[None, :, None], eidx].set(ern)
            return (w_group[:, :, None] * w_exp * SCALE).reshape(N, E)
        key = jax.random.key(seed)
        ks = jax.random.split(key, 6)
        B, T, D, H = (2, 1024, 512, 64)
        x = jax.random.normal(ks[0], (B, T, D), jnp.float32)
        Wr = jax.random.normal(ks[1], (D, G), jnp.float32) * 0.02
        br = jnp.zeros((G,), jnp.float32)
        Wgate = jax.random.normal(ks[2], (G, D, EPG), jnp.float32) * 0.02
        bgate = jnp.zeros((G, EPG), jnp.float32)
        W1 = jax.random.normal(ks[3], (E, D, H), jnp.float32) * 0.02
        W3 = jax.random.normal(ks[4], (E, D, H), jnp.float32) * 0.02
        W2 = jax.random.normal(ks[5], (E, H, D), jnp.float32) * 0.02
        return {'x': x, 'Wr': Wr, 'br': br, 'Wgate': Wgate, 'bgate': bgate, 'W1': W1, 'W3': W3, 'W2': W2}
    _L0_ffn_all = _L0_ffn_setup()
    _L0_ffn_in = {k: v for k, v in _L0_ffn_all.items() if k in ('Wr', 'br', 'Wgate', 'bgate', 'W1', 'W3', 'W2')}
    del _L0_ffn_all

    def _L1_gnn_setup():
        import jax, jax.numpy as jnp
        import numpy as np
        N_NODES = 625
        N_EDGES = 6250
        N_SEG = 16
        EXTENT = 32
        N_PATHS = 64
        OP_SIZE = N_SEG * EXTENT
        key = jax.random.key(seed)
        k1, k2, k3, k4, k5, k6 = jax.random.split(key, 6)
        x_nodes = jax.random.normal(k1, (N_NODES, OP_SIZE), dtype=jnp.float32)
        x_edges = jax.random.normal(k2, (N_EDGES, OP_SIZE), dtype=jnp.float32)
        path_coeffs = jax.random.normal(k3, (N_PATHS,), dtype=jnp.float32)
        src = jax.random.randint(k4, (N_EDGES,), 0, N_NODES, dtype=jnp.int64)
        dst = jax.random.randint(k5, (N_EDGES,), 0, N_NODES, dtype=jnp.int64)
        path_indices = jax.random.randint(k6, (N_PATHS, 3), 0, N_SEG, dtype=jnp.int64)
        return {'x_nodes': x_nodes, 'x_edges': x_edges, 'path_coeffs': path_coeffs, 'src': src, 'dst': dst, 'path_indices': path_indices}
    _L1_gnn_all = _L1_gnn_setup()
    _L1_gnn_in = {k: v for k, v in _L1_gnn_all.items() if k in ('path_coeffs', 'path_indices')}
    del _L1_gnn_all

    def _L1_ffn_setup():
        import jax, jax.numpy as jnp
        import numpy as np
        NEXPERTS = 16
        key = jax.random.key(seed)
        k1, k2, k3, k4 = jax.random.split(key, 4)
        B, S, D = (4, 64, 512)
        E, Sets, F = (16, 4, 32)
        scale = 0.02
        return {'x': jax.random.normal(k1, (B, S, D), dtype=jnp.float32), 'controller': jax.random.normal(k2, (D, E, Sets), dtype=jnp.float32) * scale, 'f1': jax.random.normal(k3, (D, E, Sets, F), dtype=jnp.float32) * scale, 'f2': jax.random.normal(k4, (E, Sets, F, D), dtype=jnp.float32) * scale}
    _L1_ffn_all = _L1_ffn_setup()
    _L1_ffn_in = {k: v for k, v in _L1_ffn_all.items() if k in ('controller', 'f1', 'f2')}
    del _L1_ffn_all
    return {'x': x, 'src': src, 'dst': dst, 'edge_attr_512': edge_attr_512, 'L0_gnn_W': _L0_gnn_in['W'], 'L0_gnn_b': _L0_gnn_in['b'], 'L0_gnn_diffusion_weights': _L0_gnn_in['diffusion_weights'], 'L0_ffn_Wr': _L0_ffn_in['Wr'], 'L0_ffn_br': _L0_ffn_in['br'], 'L0_ffn_Wgate': _L0_ffn_in['Wgate'], 'L0_ffn_bgate': _L0_ffn_in['bgate'], 'L0_ffn_W1': _L0_ffn_in['W1'], 'L0_ffn_W3': _L0_ffn_in['W3'], 'L0_ffn_W2': _L0_ffn_in['W2'], 'L1_gnn_path_coeffs': _L1_gnn_in['path_coeffs'], 'L1_gnn_path_indices': _L1_gnn_in['path_indices'], 'L1_ffn_controller': _L1_ffn_in['controller'], 'L1_ffn_f1': _L1_ffn_in['f1'], 'L1_ffn_f2': _L1_ffn_in['f2']}

def reference(x, src, dst, edge_attr_512, L0_gnn_W, L0_gnn_b, L0_gnn_diffusion_weights, L0_ffn_Wr, L0_ffn_br, L0_ffn_Wgate, L0_ffn_bgate, L0_ffn_W1, L0_ffn_W3, L0_ffn_W2, L1_gnn_path_coeffs, L1_gnn_path_indices, L1_ffn_controller, L1_ffn_f1, L1_ffn_f2):
    import jax
    import jax.numpy as jnp

    def _L0_gnn_ref(x, edge_index, W, b, diffusion_weights):
        import jax, jax.numpy as jnp
        import numpy as np
        N = 256
        D = 512
        E = 8192
        STEPS = 3
        h = x @ W + b
        row, col = (edge_index[0], edge_index[1])
        adj = jnp.zeros((N, N), dtype=h.dtype)
        adj = adj.at[row, col].set(1.0)
        adj = adj.at[col, row].set(1.0)
        adj = adj + jnp.eye(N, dtype=h.dtype)
        row_sum = adj.sum(axis=1, keepdims=True)
        adj = adj / jnp.maximum(row_sum, 1.0)
        out = diffusion_weights[0] * h
        cur = h
        for i in range(STEPS):
            cur = adj @ cur
            out = out + diffusion_weights[i + 1] * cur
        return jax.nn.relu(out)

    def _L0_ffn_ref(x, Wr, br, Wgate, bgate, W1, W3, W2):
        import jax, jax.numpy as jnp
        import numpy as np
        G = 4
        EPG = 4
        E = 16
        KG = 2
        K = 2
        GTP = 0.9
        TP = 0.9
        SCALE = 1.0 / float(np.sqrt(G))

        def _routing_weights(xf, Wr, br, Wgate, bgate):
            N = xf.shape[0]
            gp = jax.nn.softmax(xf @ Wr + br, axis=-1)
            order = jnp.argsort(-gp, axis=-1)
            sp_k = jnp.take_along_axis(gp, order, axis=-1)[:, :KG]
            idx_k = order[:, :KG]
            act = jnp.cumsum(sp_k, axis=-1) <= GTP
            act = act.at[:, 0].set(True)
            mp = sp_k * act
            rn = mp / (jnp.sum(mp, axis=-1, keepdims=True) + 1e-09)
            w_group = jnp.zeros((N, G), xf.dtype).at[jnp.arange(N)[:, None], idx_k].set(rn)
            ep = jax.nn.softmax(jnp.einsum('nd,gde->nge', xf, Wgate) + bgate, axis=-1)
            eorder = jnp.argsort(-ep, axis=-1)
            esp = jnp.take_along_axis(ep, eorder, axis=-1)[:, :, :K]
            eidx = eorder[:, :, :K]
            eact = jnp.cumsum(esp, axis=-1) <= TP
            eact = eact.at[:, :, 0].set(True)
            emp = esp * eact
            ern = emp / (jnp.sum(emp, axis=-1, keepdims=True) + 1e-09)
            w_exp = jnp.zeros((N, G, EPG), xf.dtype).at[jnp.arange(N)[:, None, None], jnp.arange(G)[None, :, None], eidx].set(ern)
            return (w_group[:, :, None] * w_exp * SCALE).reshape(N, E)
        B, T, D = x.shape
        xf = x.reshape(-1, D)
        tw = _routing_weights(xf, Wr, br, Wgate, bgate)
        out = jnp.zeros_like(xf)
        for e in range(E):
            h = jax.nn.silu(xf @ W1[e]) * (xf @ W3[e])
            out = out + tw[:, e:e + 1] * (h @ W2[e])
        return out.reshape(B, T, D)

    def _L1_gnn_ref(x_nodes, x_edges, path_coeffs, src, dst, path_indices):
        import jax, jax.numpy as jnp
        import numpy as np
        N_NODES = 625
        N_EDGES = 6250
        N_SEG = 16
        EXTENT = 32
        N_PATHS = 64
        OP_SIZE = N_SEG * EXTENT
        n_nodes = x_nodes.shape[0]
        x1 = x_nodes[src].reshape(-1, N_SEG, EXTENT)
        x2 = x_edges.reshape(-1, N_SEG, EXTENT)
        i1, i2, i3 = (path_indices[:, 0], path_indices[:, 1], path_indices[:, 2])
        contrib = path_coeffs[None, :, None] * x1[:, i1, :] * x2[:, i2, :]
        edge_out = jnp.zeros((x2.shape[0], N_SEG, EXTENT), x_nodes.dtype).at[:, i3, :].add(contrib)
        out = jnp.zeros((n_nodes, OP_SIZE), x_nodes.dtype).at[dst].add(edge_out.reshape(-1, OP_SIZE))
        return out

    def _L1_ffn_ref(x, controller, f1, f2):
        import jax, jax.numpy as jnp
        import numpy as np
        NEXPERTS = 16
        B, S, D = x.shape
        t = NEXPERTS
        grouped = x.reshape(B, S // t, t, D)
        cont_logits = jnp.einsum('bgtd,des->bgtes', grouped, controller)
        tie = jnp.linspace(0.0, 1e-06, t, dtype=x.dtype).reshape(t, 1, 1)
        cont_logits = cont_logits + tie
        cont_perm = (cont_logits == jnp.max(cont_logits, axis=-3, keepdims=True)).astype(x.dtype)
        intermediate = jnp.einsum('bgtd,desf->bgtesf', grouped, f1)
        inner = jnp.einsum('bgtesf,bgtes->bgesf', intermediate, cont_perm)
        inner = jax.nn.relu(inner)
        inter2 = jnp.einsum('bgesf,esfd->bgesd', inner, f2)
        result = jnp.einsum('bgesd,bgtes->bgtd', inter2, cont_perm)
        return result.reshape(B, S, D)
    edge_index = jnp.stack([src, dst])
    x = x + _L0_gnn_ref(_layernorm(x, axis=-1), edge_index, L0_gnn_W, L0_gnn_b, L0_gnn_diffusion_weights)
    x = x + _L0_ffn_ref(_layernorm(x, axis=-1)[None], L0_ffn_Wr, L0_ffn_br, L0_ffn_Wgate, L0_ffn_bgate, L0_ffn_W1, L0_ffn_W3, L0_ffn_W2)[0]
    x = x + _L1_gnn_ref(_layernorm(x, axis=-1), edge_attr_512, L1_gnn_path_coeffs, src, dst, L1_gnn_path_indices)
    x = x + _L1_ffn_ref(_layernorm(x, axis=-1)[None], L1_ffn_controller, L1_ffn_f1, L1_ffn_f2)[0]
    return x

_drawn_inputs = setup_inputs


def setup_inputs(seed=0):
    import zlib

    import numpy as np

    out = dict(_drawn_inputs(seed))
    spreads = {'L0_gnn_b': (0.0, 0.1),
     'L0_gnn_diffusion_weights': (0.25, 0.6),
     'L0_ffn_br': (0.0, 0.8),
     'L0_ffn_bgate': (0.0, 0.8)}
    factors = {'L0_ffn_Wr': 8.0,
     'L0_ffn_Wgate': 8.0,
     'L0_ffn_W1': 8.0,
     'L0_ffn_W3': 8.0,
     'L0_ffn_W2': 8.0,
     'L1_ffn_controller': 6.168,
     'L1_ffn_f1': 7.238,
     'L1_ffn_f2': 6.005}
    for name, (base, spread) in spreads.items():
        noise = np.random.default_rng([zlib.crc32(name.encode()), seed]).standard_normal(out[name].shape)
        drawn = base * np.exp(spread * noise) if base else spread * noise
        out[name] = jnp.asarray(drawn.astype(out[name].dtype))
    for name, factor in factors.items():
        out[name] = (out[name] * factor).astype(out[name].dtype)
    return out
```

```python
import concourse.bass as bass
from concourse import mybir
from contextlib import ExitStack


def graph_and_experts(nc, x, src, dst, edge, gnn_w, gnn_b, diff_w, wr, br, wgate, bgate,
                      w1, w3, w2, coef, paths, ctrl, f1, f2, out):
    F32, BF16, I32 = mybir.dt.float32, mybir.dt.bfloat16, mybir.dt.int32
    ALU, ACT, AX = mybir.AluOpType, mybir.ActivationFunctionType, mybir.AxisListType

    P = 128
    N, D = x.shape
    H = N // P
    KC = D // P
    E = src.shape[0]
    T = E // P
    NP = coef.shape[0]
    U = 32
    NS = D // U
    G = wr.shape[1]
    EX = wgate.shape[1]
    HC = w2.shape[0] // P
    STEPS = diff_w.shape[0] - 1
    TG = 16
    NG = N // TG
    ES = ctrl.shape[1]
    FC = f2.shape[0] // P
    EQ = ES // FC
    FE = P // EQ
    PH = P // TG

    BLOCKS = [11, 12, 11]
    FIRST = [0, 11, 23]
    PT = 4
    PU = 8
    NB = len(BLOCKS)
    BMAX = max(BLOCKS)
    LATE = FIRST[2]
    SLOTS = 4
    DR = 4
    assert sum(BLOCKS) == T

    with ExitStack() as ctx:
        def sb(name, shape, dt=F32):
            return ctx.enter_context(nc.sbuf_tensor(name, shape, dt))

        def sem(name):
            return ctx.enter_context(nc.semaphore(name))

        psum = ctx.enter_context(nc.psum_tensor("psum", [P, 8 * 512], F32))
        bank = [psum[:, i * 512:(i + 1) * 512] for i in range(8)]

        def path_sums(k):
            return psum[:, bass.ds(k * (PT * U) + 4 * 512, PT * U)]

        xs = sb("xs", [P, H, D])
        xn = sb("xn", [P, H, D])
        edges = sb("edges", [P, T, D])
        src_t = sb("src_t", [P, H, T * P], BF16)
        big = sb("big", [P, 2 * (BLOCKS[0] + BMAX) * D])
        prod = sb("prod", [P, SLOTS, BMAX, U])
        dst_oh = sb("dst_oh", [P, DR, N])
        xparts = sb("xparts", [P, 3, H, D], BF16)
        ident = sb("ident", [P, P])
        ident_b = sb("ident_b", [P, P], BF16)
        iota_b = sb("iota_b", [P, N], BF16)
        iota_f = sb("iota_f", [P, N])
        node_id = sb("node_id", [P, H])
        zero_b = sb("zero_b", [P, 512], BF16)
        coef_b = sb("coef_b", [P, NP])
        path_i = sb("path_i", [1, 3 * NP], I32)
        idx_i = sb("idx_i", [P, 2, T], I32)
        src_b = sb("src_b", [P, T], BF16)
        idx_f = sb("idx_f", [P, 2, T])
        stats = sb("stats", [P, H, 6])
        mv = sb("mv", [P, H, 2])
        rstd = sb("rstd", [P, H])
        root = sb("root", [P, H])
        eps = sb("eps", [P, 1])
        dw_b = sb("dw_b", [P, STEPS + 1])
        route_bias = sb("route_bias", [P, G + EX])
        small = prod[:].rearrange("p s t u -> p (s t u)")

        def carve(base, dt_size=4):
            at = [0]
            flat = base

            def take(shape, dt=F32):
                n = 1
                for s in shape:
                    n *= s
                words = n if dt != BF16 else (n + 1) // 2
                v = flat[:, at[0]:at[0] + words]
                at[0] += words
                assert at[0] <= flat.shape[1], (at[0], flat.shape)
                if dt != F32:
                    v = v.bitcast(dt)
                names = "abcd"[:len(shape)]
                if len(shape) > 1:
                    v = v.rearrange(f"p ({' '.join(names)}) -> p {' '.join(names)}",
                                    **{c: s for c, s in zip(names, shape)})
                return v
            return take

        take = carve(big[:, :])
        w_sb = take([KC, D])
        w1_sb = take([KC, w1.shape[1]])
        w3_sb = take([KC, w3.shape[1]])
        w2_sb = take([HC, D])
        src_oh = take([T, N], BF16)
        dst_ohb = take([T, N], BF16)
        take = carve(big[:, :])
        x1g = [take([BLOCKS[0], D]), take([BMAX, D])]
        esum = [take([BLOCKS[0], D]), take([BMAX, D])]
        late = edges[:, LATE:T, :].rearrange("p t f -> p (t f)")
        take = carve(late)
        xnT = take([KC, N])
        bias_b = take([D])
        eye = take([H, N])
        adj = take([H, N])
        cur = take([H, D])
        src_bc = [take([512], BF16), take([512], BF16)]
        link_b = take([H, N], BF16)
        rsum = take([H, 1])
        rinv = take([H, 1])
        outacc = xparts[:, 0:2].rearrange("p a h d -> p (a h d)").bitcast(F32).rearrange(
            "p (h d) -> p h d", h=H)
        take = carve(late)
        take([KC, N])
        hT = take([HC, N])
        gate = [take([N]), take([N])]
        twT = take([N])
        spread = take([HC * P])
        take = carve(edges[:, 0:LATE, :].rearrange("p t f -> p (t f)"))
        f1_sb = take([KC, f1.shape[1]])
        f2_lo = take([6, D])
        f2_hi = carve(late)([FC - 6, D])
        take = carve(big[:, :])
        xnT2 = take([KC, N])
        logit = take([N])
        tie = take([N])
        top = take([NG])
        permT = take([N])
        permT_b = take([N], BF16)
        select = take([FC * P], BF16)
        group_of = take([PH])
        perm_bd = take([H, PH, ES])
        yT = take([KC, ES, NG])
        perm_f = take([FC, N])
        inner = take([FC, NG])
        z = take([FC, N])
        tw_sb = sb("tw_sb", [P, H * EX])
        w_cat = sb("w_cat", [P, KC, G + EX])
        ctrl_sb = sb("ctrl_sb", [P, KC, ES])

        def f2_sb(c):
            return f2_lo[:, c, :] if c < 6 else f2_hi[:, c - 6, :]

        x_in, idx_in, w_in, w1_in, w3_in, w2_in = (sem(n) for n in
                                                   ("x_in", "idx_in", "w_in", "w1_in", "w3_in", "w2_in"))
        edge_in = [sem(f"edge_in{b}") for b in range(NB)]
        f1_in, f2_in, f2b_in, small_in, stored = (sem(n) for n in ("f1_in", "f2_in", "f2b_in", "small_in", "stored"))
        made = sem("made")
        const = sem("const")
        chain = sem("chain")
        var_ready, root_ready = sem("var_ready"), sem("root_ready")
        xn_ready, xnT_ps, xnT_ready = sem("xn_ready"), sem("xnT_ps"), sem("xnT_ready")
        idx_ready, onehot = sem("idx_ready"), sem("onehot")
        h_ps, h_ready = sem("h_ps"), sem("h_ready")
        bc_ps, bc_copied, bc_used = sem("bc_ps"), sem("bc_copied"), sem("bc_used")
        cnt_ps, link_ready, sym_ps, adj_ready = (sem(n) for n in ("cnt_ps", "link_ready", "sym_ps", "adj_ready"))
        diff_ps, cur_ready, cur_used = sem("diff_ps"), sem("cur_ready"), sem("cur_used")
        logit_ps, route_in, exp_done, tw_ready, twT_ps, twT_ready = (
            sem(n) for n in ("logit_ps", "route_in", "exp_done", "tw_ready", "twT_ps", "twT_ready"))
        up_ps, gated, hid, tw_ps, hid_w, down_ps, x2_ready = (
            sem(n) for n in ("up_ps", "gated", "hid", "tw_ps", "hid_w", "down_ps", "x2_ready"))
        part_a, part_r, parts_ready = sem("part_a"), sem("part_r"), sem("parts_ready")
        gat_ps, gathered = sem("gat_ps"), sem("gathered")
        cleared, mults, sums, psums = sem("cleared"), sem("mults"), sem("sums"), sem("psums")
        block_ps, block_out = sem("block_ps"), sem("block_out")
        dst_made, scattered, x3_ready = sem("dst_made"), sem("scattered"), sem("x3_ready")
        lg_ps, perm_ready, pt_ps, bd_ready, y_ps, y_even = (
            sem(n) for n in ("lg_ps", "perm_ready", "pt_ps", "bd_ready", "y_ps", "y_even"))
        y_odd = sem("y_odd")
        pf_ps, pf_ready, in_ps, in_ready, z_ready, res_ps, fin = (
            sem(n) for n in ("pf_ps", "pf_ready", "in_ps", "in_ready", "z_ready", "res_ps", "fin"))
        sel_ready = sem("sel_ready")

        block = ctx.enter_context(nc.Block())

        def halves(ap):
            return ap.rearrange("(h p) f -> p h f", p=P)

        def rows(ap):
            return ap.rearrange("(c p) n -> p c n", p=P)

        edge_v = edge.rearrange("(p t) f -> p t f", p=P)

        @block.sync
        def _(sp):
            sp.dma_start(xs[:], halves(x)).then_inc(x_in, 16)
            sp.dma_start(idx_i[:, 0], src.rearrange("(p t) -> p t", p=P)).then_inc(idx_in, 16)
            sp.dma_start(idx_i[:, 1], dst.rearrange("(p t) -> p t", p=P)).then_inc(idx_in, 16)
            sp.dma_start(w_sb, rows(gnn_w)).then_inc(w_in, 16)
            sp.dma_start(w1_sb, rows(w1)).then_inc(w1_in, 16)
            sp.dma_start(w3_sb, rows(w3)).then_inc(w3_in, 16)
            sp.dma_start(w2_sb, rows(w2)).then_inc(w2_in, 16)
            for b in range(NB - 1):
                t = FIRST[b]
                sp.dma_start(edges[:, t:t + BLOCKS[b], :], edge_v[:, t:t + BLOCKS[b], :]).then_inc(edge_in[b], 16)
            sp.wait_ge(x2_ready, H)
            sp.dma_start(edges[:, LATE:T, :], edge_v[:, LATE:T, :]).then_inc(edge_in[NB - 1], 16)
            sp.wait_ge(mults, NP * (NB - 1))
            sp.dma_start(f1_sb, rows(f1)).then_inc(f1_in, 16)
            sp.dma_start(f2_lo, rows(f2)[:, 0:6, :]).then_inc(f2_in, 16)
            sp.wait_ge(mults, NP * NB)
            sp.dma_start(f2_hi, rows(f2)[:, 6:FC, :]).then_inc(f2b_in, 16)
            for h in range(H):
                sp.wait_ge(fin, h + 1)
                sp.dma_start(halves(out)[:, h, :], xs[:, h, :]).then_inc(stored, 16)
            sp.wait_ge(stored, 16 * H)

        @block.gpsimd
        def _(pool):
            def eye_of(ap, base, made_at):
                pool.wait_ge(made, made_at)
                return nc.gpsimd.affine_select(out=ap, in_=ap, compare_op=ALU.not_equal, fill=1.0, base=base,
                                               pattern=[[-1, ap.shape[-1]]], channel_multiplier=1)
            nc.gpsimd.memset(ident[:], 0.0).then_inc(made, 1)
            nc.gpsimd.memset(ident_b[:], 0.0).then_inc(made, 1)
            nc.gpsimd.memset(eye, 0.0).then_inc(made, 1)
            nc.gpsimd.memset(zero_b[:], 0.0).then_inc(const, 1)
            nc.gpsimd.iota(iota_b[:], pattern=[[1, N]], base=0, channel_multiplier=0,
                           allow_small_or_imprecise_dtypes=True).then_inc(const, 1)
            nc.gpsimd.iota(iota_f[:], pattern=[[1, N]], base=0, channel_multiplier=0,
                           allow_small_or_imprecise_dtypes=True).then_inc(const, 1)
            nc.gpsimd.iota(node_id[:], pattern=[[P, H]], base=0, channel_multiplier=1,
                           allow_small_or_imprecise_dtypes=True).then_inc(const, 1)
            nc.gpsimd.memset(eps[:], 1e-5).then_inc(const, 1)
            eye_of(ident[:], 0, 1).then_inc(const, 1)
            eye_of(ident_b[:], 0, 2).then_inc(const, 1)
            for h in range(H):
                eye_of(eye[:, h, :], P * h, 3).then_inc(const, 1)

            pool.wait_ge(xn_ready, 2 * H)
            nc.gpsimd.memset(spread[0:EX, :], 0.0).then_inc(made, 1)
            pool.wait_ge(made, 4)
            sp_v = spread[0:EX, :].rearrange("k (e j) -> k e j", e=EX)
            nc.gpsimd.affine_select(out=sp_v, in_=sp_v, compare_op=ALU.not_equal, fill=1.0, base=0,
                                    pattern=[[-1, EX], [0, HC * P // EX]], channel_multiplier=1).then_inc(sel_ready, 1)

            def clear(b):
                if b == 0:
                    pool.wait_ge(x2_ready, H)
                if b >= 2:
                    pool.wait_ge(scattered, FIRST[b - 1])
                nc.gpsimd.memset(esum[b % 2][:, PT:BLOCKS[b], :], 0.0).then_inc(cleared, 1)

            clear(0)
            clear(1)
            for b in range(NB):
                for t in range(FIRST[b], FIRST[b] + BLOCKS[b]):
                    if t >= DR:
                        pool.wait_ge(scattered, t - DR + 1)
                    nc.gpsimd.tensor_scalar(dst_oh[:, t % DR, :], iota_f[:], idx_f[:, 1, t:t + 1], None,
                                            ALU.is_equal).then_inc(dst_made, 1)
                if b + 2 < NB:
                    clear(b + 2)

            pool.wait_ge(x3_ready, H)
            nc.gpsimd.memset(select[0:ES, :], 0.0).then_inc(made, 1)
            nc.gpsimd.memset(group_of, 1.0).then_inc(made, 1)
            nc.gpsimd.iota(tie[0:ES, :].rearrange("p (g t) -> p g t", t=TG), pattern=[[0, NG], [1, TG]], base=0,
                           channel_multiplier=0, allow_small_or_imprecise_dtypes=True).then_inc(sel_ready, 1)
            pool.wait_ge(made, 6)
            nc.gpsimd.affine_select(out=group_of, in_=group_of, compare_op=ALU.is_ge, fill=0.0, base=0,
                                    pattern=[[-TG, PH]], channel_multiplier=1).then_inc(made, 1)
            pool.wait_ge(made, 7)
            nc.gpsimd.affine_select(out=group_of, in_=group_of, compare_op=ALU.is_ge, fill=0.0, base=TG - 1,
                                    pattern=[[TG, PH]], channel_multiplier=-1).then_inc(sel_ready, 1)
            se_v = select[0:ES, :].rearrange("k (e j) -> k e j", e=ES)
            nc.gpsimd.affine_select(out=se_v, in_=se_v, compare_op=ALU.not_equal, fill=1.0, base=0,
                                    pattern=[[-1, ES], [0, FE]], channel_multiplier=1).then_inc(sel_ready, 1)

        @block.scalar
        def _(act):
            act.dma_start(bias_b, gnn_b.rearrange("(o n) -> o n", o=1).broadcast_to([P, D])).then_inc(small_in, 16)
            act.dma_start(dw_b[:], diff_w.rearrange("(o n) -> o n", o=1).broadcast_to([P, STEPS + 1])).then_inc(small_in, 16)
            act.dma_start(route_bias[:, 0:G], br.rearrange("(o n) -> o n", o=1).broadcast_to([P, G])).then_inc(small_in, 16)
            act.dma_start(route_bias[:, G:], bgate.rearrange("(o n) -> o n", o=1).broadcast_to([P, EX])).then_inc(small_in, 16)
            act.dma_start(w_cat[:, :, 0:G], rows(wr)).then_inc(small_in, 16)
            act.dma_start(w_cat[:, :, G:], rows(wgate)).then_inc(small_in, 16)
            act.dma_start(ctrl_sb[:], rows(ctrl)).then_inc(small_in, 16)
            act.dma_start(coef_b[:], coef.rearrange("(o n) -> o n", o=1).broadcast_to([P, NP])).then_inc(small_in, 16)
            act.dma_start(path_i[:], paths.rearrange("(o n) k -> o (n k)", o=1)).then_inc(small_in, 16)

            def root_of_variance(n):
                act.wait_ge(var_ready, H * (n + 1))
                nc.scalar.activation(root[:], mv[:, :, 1], ACT.Sqrt, bias=eps[:]).then_inc(root_ready, 1)

            def copy_xnT(stage, to):
                act.wait_ge(xnT_ps, 2 * stage + 1)
                nc.scalar.activation(to[:, 0:2, :].rearrange("p c n -> p (c n)"), bank[0], ACT.Copy)\
                    .then_inc(xnT_ready, 1)

            act.wait_ge(const, 5)
            root_of_variance(0)
            copy_xnT(0, xnT)
            for q in range(-(-T // 4)):
                n = min(4, T - 4 * q) * P
                act.wait_ge(bc_ps, q + 1)
                if q >= 2:
                    act.wait_ge(bc_used, q - 1)
                nc.scalar.activation(src_bc[q % 2][:, 0:n], bank[6 + q % 2][:, 0:n], ACT.Copy).then_inc(bc_copied, 1)
            act.wait_ge(adj_ready, 1)
            for s in range(STEPS):
                act.wait_ge(diff_ps, H * (s + 1))
                act.wait_ge(cur_used, H * (s + 1))
                for h in range(H):
                    nc.scalar.activation(cur[:, h, :], bank[(4, 2)[s % 2] + h], ACT.Copy,
                                         scale=rinv[:, h, :]).then_inc(cur_ready, 1)

            root_of_variance(1)
            copy_xnT(1, xnT)
            act.wait_ge(route_in, 1)
            nc.scalar.activation(small[:, 0:40], small[:, 0:40], ACT.Exp).then_inc(exp_done, 1)
            for c in range(HC):
                act.wait_ge(up_ps, c + 1)
                if c >= 2:
                    act.wait_ge(hid, c - 1)
                nc.scalar.activation(gate[c % 2], bank[2 + c % 4][:, 0:N], ACT.Silu).then_inc(gated, 1)

            root_of_variance(2)
            act.wait_ge(xn_ready, 3 * H)
            nc.scalar.activation(xparts[:, 0], xn[:], ACT.Copy).then_inc(part_a, 1)
            act.wait_ge(part_r, 1)
            nc.scalar.activation(xparts[:, 1], xn[:], ACT.Copy).then_inc(part_a, 1)
            act.wait_ge(part_r, 2)
            nc.scalar.activation(xparts[:, 2], xn[:], ACT.Copy).then_inc(part_a, 1)

            def copy_gathered(b):
                for t in range(FIRST[b], FIRST[b] + BLOCKS[b]):
                    act.wait_ge(gat_ps, t + 1)
                    if b >= 2 and t == FIRST[b]:
                        act.wait_ge(mults, NP * (b - 1))
                    nc.scalar.activation(x1g[b % 2][:, t - FIRST[b], :], bank[t % 2], ACT.Copy).then_inc(gathered, 1)

            copy_gathered(0)
            for b in range(NB):
                if b + 1 < NB:
                    copy_gathered(b + 1)
                if b >= 2:
                    act.wait_ge(scattered, FIRST[b - 1])
                for q in range(4):
                    act.wait_ge(block_ps, 4 * b + q + 1)
                    nc.scalar.activation(
                        esum[b % 2][:, 0:PT, q * P:(q + 1) * P].rearrange("p t (k u) -> p k t u", u=U),
                        bank[4 + q].rearrange("p (k t u) -> p k t u", t=PT, u=U), ACT.Copy).then_inc(block_out, 1)

            root_of_variance(3)
            copy_xnT(2, xnT2)
            for j in range(FC // 2):
                act.wait_ge(pf_ps, j + 1)
                nc.scalar.activation(perm_f[:, 2 * j:2 * j + 2, :].rearrange("p c n -> p (c n)"), bank[6 + j % 2],
                                     ACT.Copy).then_inc(pf_ready, 1)
            for i in range(0, 2 * KC, 2):
                act.wait_ge(y_ps, i + 1)
                nc.scalar.activation(yT[:, i // 2, :, 0:PH].rearrange("p e g -> p g e"),
                                     bank[i % 4].rearrange("p (g e) -> p g e", e=ES), ACT.Copy).then_inc(y_even, 1)
            act.wait_ge(in_ps, 1)
            for q in range(2):
                for k in range(2):
                    nc.scalar.activation(
                        inner[FE * q:FE * (q + 1), 8 * k:8 * k + 8, :],
                        bank[4 + k][FE * q:FE * (q + 1), :].rearrange("p (c e g) -> p c e g", e=EQ, g=NG)[:, :, q, :],
                        ACT.Relu).then_inc(in_ready, 1)

        @block.vector
        def _(dve):
            links = [0]
            lns = [0]

            def link(ins):
                links[0] += 1
                ins.then_inc(chain, 1)
                dve.wait_ge(chain, links[0])

            def layer_norm():
                for h in range(H):
                    link(nc.vector.bn_stats(out=stats[:, h, :], in_=xs[:, h, :]))
                    nc.vector.bn_aggr(out=mv[:, h, :], in_=stats[:, h, :]).then_inc(var_ready, 1)
                lns[0] += 1
                dve.wait_ge(root_ready, lns[0])
                link(nc.vector.reciprocal(rstd[:], root[:]))
                for h in range(H):
                    nc.vector.tensor_scalar(xn[:, h, :], xs[:, h, :], mv[:, h, 0:1], rstd[:, h:h + 1],
                                            ALU.subtract, ALU.mult).then_inc(xn_ready, 1)

            def copy_xnT(stage, to):
                dve.wait_ge(xnT_ps, 2 * stage + 2)
                nc.vector.tensor_copy(to[:, 2:4, :].rearrange("p c n -> p (c n)"), bank[1]).then_inc(xnT_ready, 1)

            dve.wait_ge(x_in, 16)
            layer_norm()
            dve.wait_ge(idx_in, 32)
            nc.vector.tensor_copy(idx_f[:], idx_i[:]).then_inc(idx_ready, 1)
            nc.vector.tensor_copy(src_b[:], idx_i[:, 0]).then_inc(idx_ready, 1)
            copy_xnT(0, xnT)
            dve.wait_ge(idx_ready, 2)
            dve.wait_ge(const, 4)
            for t in range(T):
                nc.vector.tensor_scalar(src_oh[:, t, :], iota_b[:], idx_f[:, 0, t:t + 1], None, ALU.is_equal)\
                    .then_inc(onehot, 1)
                nc.vector.tensor_scalar(dst_ohb[:, t, :], iota_b[:], idx_f[:, 1, t:t + 1], None, ALU.is_equal)\
                    .then_inc(onehot, 1)
            dve.wait_ge(small_in, 16 * 9)
            for h in range(H):
                dve.wait_ge(h_ps, h + 1)
                nc.vector.tensor_tensor(cur[:, h, :], bank[2 + h], bias_b, ALU.add).then_inc(h_ready, 1)
            for q in range(-(-T // 4)):
                n = min(4, T - 4 * q) * P
                dve.wait_ge(bc_copied, q + 1)
                for h in range(H):
                    last = nc.vector.tensor_scalar(src_t[:, h, q * 512:q * 512 + n], src_bc[q % 2][:, 0:n],
                                                   node_id[:, h:h + 1], None, ALU.is_equal)
                    if h == 0:
                        link(last)
                last.then_inc(bc_used, 1)
            for h in range(H):
                dve.wait_ge(cnt_ps, h + 1)
                nc.vector.tensor_scalar(link_b[:, h, :], bank[4 + h][:, 0:N], 0.5, None, ALU.is_gt).then_inc(link_ready, 1)
            dve.wait_ge(sym_ps, 1)
            for h in range(H):
                link(nc.vector.scalar_tensor_tensor(out=adj[:, h, :], in0=bank[6][:, h * N:(h + 1) * N], scalar=0.5,
                                                    in1=eye[:, h, :], op0=ALU.is_gt, op1=ALU.add,
                                                    accum_out=rsum[:, h, :]))
            link(nc.vector.tensor_scalar(rsum, rsum, 1.0, None, ALU.max))
            nc.vector.reciprocal(rinv, rsum).then_inc(adj_ready, 1)
            dve.wait_ge(h_ready, H)
            for h in range(H):
                nc.vector.tensor_scalar(outacc[:, h, :], cur[:, h, :], dw_b[:, 0:1], None, ALU.mult).then_inc(cur_used, 1)
            for s in range(STEPS):
                for h in range(H):
                    dve.wait_ge(cur_ready, H * s + h + 1)
                    dve.wait_ge(cur_used, H * s + h + 1)
                    nc.vector.scalar_tensor_tensor(out=outacc[:, h, :], in0=cur[:, h, :], scalar=dw_b[:, s + 1:s + 2],
                                                   in1=outacc[:, h, :], op0=ALU.mult, op1=ALU.add).then_inc(cur_used, 1)
            for h in range(H):
                dve.wait_ge(cur_used, H * STEPS + h + 1)
                link(nc.vector.scalar_tensor_tensor(out=xs[:, h, :], in0=outacc[:, h, :], scalar=0.0,
                                                    in1=xs[:, h, :], op0=ALU.max, op1=ALU.add))

            layer_norm()
            copy_xnT(1, xnT)
            R = H * (1 + G)
            sm = [0]

            def room(n):
                v = small[:, sm[0]:sm[0] + n]
                sm[0] += n
                return v
            prob = room(R * G)
            p2 = prob.rearrange("p (r k) -> p r k", k=G)
            dve.wait_ge(logit_ps, 1)
            link(nc.vector.tensor_tensor(prob.rearrange("p (h k) -> p h k", h=H),
                                         bank[6][:, 0:R * G].rearrange("p (h k) -> p h k", h=H),
                                         route_bias[:].rearrange("p (o k) -> p o k", o=1).broadcast_to([P, H, G + EX]), ALU.add))
            mx = room(R).rearrange("p (r o) -> p r o", o=1)
            link(nc.vector.tensor_reduce(mx, p2, AX.X, ALU.max))
            nc.vector.tensor_tensor(p2, p2, mx.broadcast_to([P, R, G]), ALU.subtract).then_inc(route_in, 1)
            dve.wait_ge(exp_done, 1)
            link(nc.vector.tensor_reduce(mx, p2, AX.X, ALU.add))
            link(nc.vector.reciprocal(mx, mx))
            link(nc.vector.tensor_tensor(p2, p2, mx.broadcast_to([P, R, G]), ALU.mult))
            def pairs():
                return room(R * G * G).rearrange("p (r i j) -> p r i j", i=G, j=G)
            gt, eq = pairs(), pairs()
            low = room(G * G).rearrange("p (i j) -> p i j", j=G)
            for i in range(G):
                for j in range(G):
                    last = nc.vector.memset(low[:, i, j:j + 1], 1.0 if j < i else 0.0)
            link(last)
            pj = p2.rearrange("p r (o k) -> p r o k", o=1).broadcast_to([P, R, G, G])
            pi = p2.rearrange("p r (k o) -> p r k o", o=1).broadcast_to([P, R, G, G])
            link(nc.vector.tensor_tensor(gt, pj, pi, ALU.is_gt))
            link(nc.vector.tensor_tensor(eq, pj, pi, ALU.is_equal))
            link(nc.vector.tensor_tensor(
                eq.rearrange("p r i j -> p r (i j)"), eq.rearrange("p r i j -> p r (i j)"),
                low.rearrange("p (o i) j -> p o (i j)", o=1).broadcast_to([P, R, G * G]), ALU.mult))
            link(nc.vector.tensor_tensor(gt, gt, eq, ALU.add))
            rank = room(R * G).rearrange("p (r k) -> p r k", k=G)
            link(nc.vector.tensor_reduce(rank.rearrange("p r (k o) -> p r k o", o=1), gt, AX.X, ALU.add))
            first, second = (room(R * G).rearrange("p (r k) -> p r k", k=G) for _ in range(2))
            s1, s2, keep = (room(R).rearrange("p (r o) -> p r o", o=1) for _ in range(3))
            link(nc.vector.scalar_tensor_tensor(out=first, in0=rank, scalar=0.0, in1=p2, op0=ALU.is_equal, op1=ALU.mult))
            link(nc.vector.scalar_tensor_tensor(out=second, in0=rank, scalar=1.0, in1=p2, op0=ALU.is_equal, op1=ALU.mult))
            link(nc.vector.tensor_reduce(s1, first, AX.X, ALU.add))
            link(nc.vector.tensor_reduce(s2, second, AX.X, ALU.add))
            link(nc.vector.tensor_tensor(keep, s1, s2, ALU.add))
            link(nc.vector.tensor_scalar(keep, keep, 0.9, None, ALU.is_le))
            link(nc.vector.tensor_tensor(s2, s2, keep, ALU.mult))
            link(nc.vector.tensor_tensor(second, second, keep.broadcast_to([P, R, G]), ALU.mult))
            link(nc.vector.tensor_tensor(first, first, second, ALU.add))
            link(nc.vector.scalar_tensor_tensor(out=s1, in0=s1, scalar=1e-9, in1=s2, op0=ALU.add, op1=ALU.add))
            link(nc.vector.reciprocal(s1, s1))
            link(nc.vector.tensor_tensor(first, first, s1.broadcast_to([P, R, G]), ALU.mult))
            tw = tw_sb[:].rearrange("p (h g k) -> p h g k", h=H, g=G)
            fh = first.rearrange("p (h r) k -> p h r k", h=H)
            for h in range(H):
                nc.vector.scalar_tensor_tensor(
                    out=tw[:, h], in0=fh[:, h, 0, :].rearrange("p (k o) -> p k o", o=1).broadcast_to([P, G, G]),
                    scalar=float(G) ** -0.5, in1=fh[:, h, 1:, :], op0=ALU.mult, op1=ALU.mult).then_inc(tw_ready, 1)

            def hidden(c):
                dve.wait_ge(gated, c + 1)
                nc.vector.tensor_tensor(hT[:, c, :], gate[c % 2], bank[2 + c % 4][:, N:2 * N], ALU.mult).then_inc(hid, 1)

            dve.wait_ge(twT_ps, 1)
            nc.vector.tensor_copy(twT[0:EX, :], bank[7][0:EX, 0:N]).then_inc(twT_ready, 1)
            for c in range(HC):
                hidden(c)
            for j in range(HC // 2):
                dve.wait_ge(tw_ps, j + 1)
                dve.wait_ge(hid, 2 * j + 2)
                v = hT[:, 2 * j:2 * j + 2, :].rearrange("p c n -> p (c n)")
                nc.vector.tensor_tensor(v, v, bank[(0, 1, 6, 7)[j]], ALU.mult).then_inc(hid_w, 1)
            for h in range(H):
                dve.wait_ge(down_ps, h + 1)
                nc.vector.tensor_tensor(xs[:, h, :], xs[:, h, :], bank[2 + h], ALU.add).then_inc(x2_ready, 1)

            dve.wait_ge(x2_ready, H)
            layer_norm()
            dve.wait_ge(part_a, 1)
            dve.wait_ge(xn_ready, 3 * H)
            nc.vector.tensor_tensor(xn[:], xn[:], xparts[:, 0], ALU.subtract).then_inc(part_r, 1)
            dve.wait_ge(part_a, 2)
            dve.wait_ge(part_r, 1)
            nc.vector.tensor_tensor(xn[:], xn[:], xparts[:, 1], ALU.subtract).then_inc(part_r, 1)

            dve.wait_ge(part_a, 3)
            nc.vector.memset(prod[:, :, 0:1, 0:1], 0.0).then_inc(sums, SLOTS)
            regs = [dve.alloc_register(f"path{i}") for i in range(3 * PU)]
            for b in range(NB):
                tiles, p0 = BLOCKS[b], NP * b
                xg, es = x1g[b % 2], esum[b % 2]
                dve.wait_ge(gathered, FIRST[b] + tiles)
                dve.wait_ge(edge_in[b], 16)
                dve.wait_ge(cleared, b + 1)
                dve.load(regs, path_i[0:1, 0:3 * PU])
                with dve.Fori(0, NP // PU) as turn:
                    def segment(j, k):
                        return bass.ds(dve.snap(regs[3 * j + k], min_val=0, max_val=NS - 1) * U, U)

                    def multiply(j):
                        n = p0 + turn * PU + j
                        i1, i2 = segment(j, 0), segment(j, 1)
                        dve.wait_ge(sums, n + 1)
                        dve.wait_ge(psums, n + 1)
                        nc.vector.scalar_tensor_tensor(
                            out=prod[:, j % SLOTS, 0:tiles], in0=xg[:, 0:tiles, i1],
                            scalar=coef_b[:, bass.ds(turn * PU + j, 1)],
                            in1=edges[:, FIRST[b]:FIRST[b] + tiles, i2], op0=ALU.mult, op1=ALU.mult).then_inc(mults, 1)

                    def add(j, to):
                        n = p0 + turn * PU + j
                        dve.wait_ge(mults, n + 1)
                        dve.wait_ge(sums, n + SLOTS)
                        v = es[:, PT:tiles, to]
                        nc.vector.tensor_tensor(v, v, prod[:, j % SLOTS, PT:tiles], ALU.add).then_inc(sums, 1)

                    multiply(0)
                    for j in range(PU):
                        if j + 1 < PU:
                            multiply(j + 1)
                        to = segment(j, 2)
                        if j + 1 == PU:
                            nxt = (turn * PU + PU) % NP
                            dve.load(regs, path_i[0:1, bass.ds(nxt * 3, 3 * PU)])
                        add(j, to)
            for h in range(H):
                dve.wait_ge(scattered, T)
                nc.vector.tensor_tensor(xs[:, h, :], xs[:, h, :], bank[2 + h], ALU.add).then_inc(x3_ready, 1)

            dve.wait_ge(x3_ready, H)
            layer_norm()
            copy_xnT(2, xnT2)
            dve.wait_ge(sel_ready, 4)
            dve.wait_ge(lg_ps, 1)
            link(nc.vector.scalar_tensor_tensor(out=logit[0:ES, :], in0=tie[0:ES, :], scalar=1e-6 / (TG - 1),
                                                in1=bank[4][0:ES, 0:N], op0=ALU.mult, op1=ALU.add))
            lg = logit[0:ES, :].rearrange("p (g t) -> p g t", t=TG)
            tp = top[0:ES, :].rearrange("p (g o) -> p g o", o=1)
            link(nc.vector.tensor_reduce(tp, lg, AX.X, ALU.max))
            link(nc.vector.tensor_tensor(permT[0:ES, :].rearrange("p (g t) -> p g t", t=TG), lg,
                                         tp.broadcast_to([ES, NG, TG]), ALU.is_equal))
            nc.vector.tensor_copy(permT_b[0:ES, :], permT[0:ES, :]).then_inc(perm_ready, 1)
            for h in range(H):
                dve.wait_ge(pt_ps, H)
                nc.vector.tensor_tensor(
                    perm_bd[:, h], bank[5][:, h * ES:(h + 1) * ES].rearrange("p (o e) -> p o e", o=1).broadcast_to([P, PH, ES]),
                    group_of.rearrange("p (g o) -> p g o", o=1).broadcast_to([P, PH, ES]), ALU.mult).then_inc(bd_ready, 1)
            for i in range(1, 2 * KC, 2):
                dve.wait_ge(y_ps, i + 1)
                nc.vector.tensor_copy(yT[:, i // 2, :, PH:].rearrange("p e g -> p g e"),
                                      bank[i % 4].rearrange("p (g e) -> p g e", e=ES)).then_inc(y_odd, 1)
            dve.wait_ge(in_ps, 1)
            for q in range(2, EQ):
                for k in range(2):
                    nc.vector.tensor_scalar(
                        inner[FE * q:FE * (q + 1), 8 * k:8 * k + 8, :],
                        bank[4 + k][FE * q:FE * (q + 1), :].rearrange("p (c e g) -> p c e g", e=EQ, g=NG)[:, :, q, :],
                        0.0, None, ALU.max).then_inc(in_ready, 1)
            dve.wait_ge(in_ready, 8)
            dve.wait_ge(pf_ready, FC // 2)
            for j in range(FC // 2):
                nc.vector.tensor_tensor(
                    z[:, 2 * j:2 * j + 2, :].rearrange("p c (g t) -> p (c g) t", t=TG),
                    perm_f[:, 2 * j:2 * j + 2, :].rearrange("p c (g t) -> p (c g) t", t=TG),
                    inner[:, 2 * j:2 * j + 2, :].rearrange("p c (g o) -> p (c g) o", o=1).broadcast_to([P, 2 * NG, TG]),
                    ALU.mult).then_inc(z_ready, 1)
            for h in range(H):
                dve.wait_ge(res_ps, h + 1)
                nc.vector.tensor_tensor(xs[:, h, :], xs[:, h, :], bank[6 + h], ALU.add).then_inc(fin, 1)

        @block.tensor
        def _(pe):
            mm = nc.tensor.matmul

            def transpose_xn(stage):
                pe.wait_ge(xn_ready, H * (stage + 1 if stage < 2 else 4))
                for half in range(2):
                    for kc in (2 * half, 2 * half + 1):
                        for h in range(H):
                            last = nc.tensor.transpose(bank[half][:, (kc % 2) * N + h * P:(kc % 2) * N + (h + 1) * P],
                                                       xn[:, h, kc * P:(kc + 1) * P], ident[:])
                    last.then_inc(xnT_ps, 1)
                pe.wait_ge(xnT_ready, 2 * (stage + 1))

            pe.wait_ge(const, 5 + 2 + H)
            transpose_xn(0)
            pe.wait_ge(w_in, 16)
            for h in range(H):
                for kc in range(KC):
                    last = mm(bank[2 + h], xnT[:, kc, h * P:(h + 1) * P], w_sb[:, kc, :], start=kc == 0, stop=kc == KC - 1)
                last.then_inc(h_ps, 1)
            pe.wait_ge(idx_ready, 2)
            for q in range(-(-T // 4)):
                if q >= 2:
                    pe.wait_ge(bc_copied, q - 1)
                for t in range(4 * q, min(4 * q + 4, T)):
                    last = mm(bank[6 + q % 2][:, (t % 4) * P:(t % 4 + 1) * P], src_b[:, t:t + 1].broadcast_to([P, P]),
                              ident_b[:], start=True, stop=True)
                last.then_inc(bc_ps, 1)
            pe.wait_ge(onehot, 2 * T)
            for h in range(H):
                for t in range(T):
                    last = mm(bank[4 + h][:, 0:N], src_oh[:, t, h * P:(h + 1) * P], dst_ohb[:, t, :], start=t == 0, stop=t == T - 1)
                last.then_inc(cnt_ps, 1)
            pe.wait_ge(bc_copied, -(-T // 4))
            pe.wait_ge(link_ready, H)
            for h in range(H):
                for c in range(H):
                    o = bank[6][:, h * N + c * P:h * N + (c + 1) * P]
                    mm(o, ident_b[:], link_b[:, h, c * P:(c + 1) * P], start=True, stop=False)
                    last = mm(o, link_b[:, c, h * P:(h + 1) * P], ident_b[:], start=False, stop=True)
            last.then_inc(sym_ps, 1)
            pe.wait_ge(adj_ready, 1)
            pe.wait_ge(h_ready, H)
            for s in range(STEPS):
                if s:
                    pe.wait_ge(cur_ready, H * s)
                for h in range(H):
                    for c in range(H):
                        last = mm(bank[(4, 2)[s % 2] + h], adj[:, c, h * P:(h + 1) * P], cur[:, c, :], start=c == 0, stop=c == H - 1)
                    last.then_inc(diff_ps, 1)

            transpose_xn(1)
            for h in range(H):
                for kc in range(KC):
                    last = mm(bank[6][:, h * (G + EX):(h + 1) * (G + EX)], xnT[:, kc, h * P:(h + 1) * P], w_cat[:, kc, :],
                              start=kc == 0, stop=kc == KC - 1)
            last.then_inc(logit_ps, 1)
            pe.wait_ge(w1_in, 16)
            pe.wait_ge(w3_in, 16)
            for c in range(HC):
                if c >= 4:
                    pe.wait_ge(hid, c - 3)
                for n, w in enumerate((w1_sb, w3_sb)):
                    for kc in range(KC):
                        last = mm(bank[2 + c % 4][:, n * N:(n + 1) * N], w[:, kc, c * P:(c + 1) * P], xnT[:, kc, :],
                                  start=kc == 0, stop=kc == KC - 1)
                last.then_inc(up_ps, 1)
                if c == 3:
                    pe.wait_ge(tw_ready, H)
                    for h in range(H):
                        last = nc.tensor.transpose(bank[7][0:EX, h * P:(h + 1) * P], tw_sb[:, h * EX:(h + 1) * EX], ident[:])
                    last.then_inc(twT_ps, 1)
            pe.wait_ge(twT_ready, 1)
            pe.wait_ge(sel_ready, 1)
            for j in range(HC // 2):
                for c in (2 * j, 2 * j + 1):
                    last = mm(bank[(0, 1, 6, 7)[j]][:, (c % 2) * N:(c % 2 + 1) * N], spread[0:EX, c * P:(c + 1) * P], twT[0:EX, :],
                              start=True, stop=True)
                last.then_inc(tw_ps, 1)
            pe.wait_ge(w2_in, 16)
            for h in range(H):
                for c in range(HC):
                    if h == 0 and c % 2 == 0:
                        pe.wait_ge(hid_w, c // 2 + 1)
                    last = mm(bank[2 + h], hT[:, c, h * P:(h + 1) * P], w2_sb[:, c, :], start=c == 0, stop=c == HC - 1)
                last.then_inc(down_ps, 1)

            def gather(t):
                if t >= 2:
                    pe.wait_ge(gathered, t - 1)
                for h in range(H):
                    for k in range(3):
                        last = mm(bank[t % 2], src_t[:, h, t * P:(t + 1) * P], xparts[:, k, h, :],
                                  start=h == 0 and k == 0, stop=h == H - 1 and k == 2)
                last.then_inc(gat_ps, 1)

            def scatter(b, t):
                pe.wait_ge(dst_made, t + 1)
                for h in range(H):
                    last = mm(bank[2 + h], dst_oh[:, t % DR, h * P:(h + 1) * P], esum[b % 2][:, t - FIRST[b], :],
                              start=t == 0, stop=t == T - 1)
                last.then_inc(scattered, 1)

            pe.wait_ge(part_a, 3)
            pe.wait_ge(x2_ready, H)
            for t in range(BLOCKS[0]):
                gather(t)
            regs = [pe.alloc_register(f"to{i}") for i in range(3 * PU)]
            for b in range(NB):
                gathers = list(range(FIRST[b + 1], FIRST[b + 1] + BLOCKS[b + 1])) if b + 1 < NB else []
                scatters = list(range(FIRST[b - 1], FIRST[b])) if b else []
                if b:
                    pe.wait_ge(block_out, 4 * b)
                    pe.wait_ge(sums, SLOTS + NP * b)
                for q in range(4):
                    last = mm(bank[4 + q], zero_b[:, 0:P], zero_b[:], start=True, stop=False)
                    if b == 0:
                        last.then_inc(psums, 1)
                for turn in range(NP // PU):
                    pe.load(regs, path_i[0:1, turn * PU * 3:(turn + 1) * PU * 3])
                    for j in range(PU):
                        n = NP * b + turn * PU + j
                        to = pe.snap(regs[3 * j + 2], min_val=0, max_val=NS - 1)
                        pe.wait_ge(mults, n + 1)
                        mm(path_sums(to), ident[:], prod[:, j % SLOTS, 0:PT].rearrange("p t u -> p (t u)"),
                           start=False, stop=False, skip_group_check=True).then_inc(psums, 1)
                        if j % 4 == 3 and gathers:
                            gather(gathers.pop(0))
                        if j % 4 == 1 and scatters:
                            scatter(b - 1, scatters.pop(0))
                assert not gathers and not scatters
                for q in range(4):
                    mm(bank[4 + q], zero_b[:, 0:P], zero_b[:], start=False, stop=True).then_inc(block_ps, 1)
            pe.wait_ge(block_out, 4 * NB)
            pe.wait_ge(sums, SLOTS + NP * NB)
            for t in range(FIRST[NB - 1], T):
                scatter(NB - 1, t)

            transpose_xn(2)
            for kc in range(KC):
                last = mm(bank[4][0:ES, 0:N], ctrl_sb[:, kc, :], xnT2[:, kc, :], start=kc == 0, stop=kc == KC - 1)
            last.then_inc(lg_ps, 1)
            pe.wait_ge(perm_ready, 1)
            for h in range(H):
                nc.tensor.transpose(bank[5][:, h * ES:(h + 1) * ES], permT[0:ES, h * P:(h + 1) * P], ident[0:ES, 0:ES])\
                    .then_inc(pt_ps, 1)
            for j in range(FC // 2):
                if j >= 2:
                    pe.wait_ge(pf_ready, j - 1)
                for c in (2 * j, 2 * j + 1):
                    last = mm(bank[6 + j % 2][:, (c % 2) * N:(c % 2 + 1) * N], select[0:ES, c * P:(c + 1) * P], permT_b[0:ES, :],
                              start=True, stop=True)
                last.then_inc(pf_ps, 1)
            pe.wait_ge(bd_ready, H)
            for i in range(2 * KC):
                if i >= 4:
                    pe.wait_ge((y_even, y_odd)[i % 2], (i - 4) // 2 + 1)
                mm(bank[i % 4], xn[:, i % 2, (i // 2) * P:(i // 2 + 1) * P], perm_bd[:, i % 2].rearrange("p g e -> p (g e)"),
                   start=True, stop=True).then_inc(y_ps, 1)
            pe.wait_ge(y_even, KC)
            pe.wait_ge(y_odd, KC)
            pe.wait_ge(f1_in, 16)
            for c in range(FC):
                for kc in range(KC):
                    last = mm(bank[4 + c // 8][:, (c % 8) * EQ * NG:(c % 8 + 1) * EQ * NG], f1_sb[:, kc, c * P:(c + 1) * P],
                              yT[:, kc, c * EQ:(c + 1) * EQ, :].rearrange("p e g -> p (e g)"), start=kc == 0, stop=kc == KC - 1)
            last.then_inc(in_ps, 1)
            pe.wait_ge(pf_ready, FC // 2)
            pe.wait_ge(f2_in, 16)
            pe.wait_ge(f2b_in, 16)
            for h in range(H):
                for c in range(FC):
                    if h == 0 and c % 2 == 0:
                        pe.wait_ge(z_ready, c // 2 + 1)
                    last = mm(bank[6 + h], z[:, c, h * P:(h + 1) * P], f2_sb(c), start=c == 0, stop=c == FC - 1)
                last.then_inc(res_ps, 1)


def kernel(**inputs):
    import numpy as np
    import concourse.bacc as bacc
    from concourse.bass_utils import run_bass_kernel_spmd

    a = {k: np.asarray(v) for k, v in inputs.items()}
    E, D, HID = a["L0_ffn_W1"].shape
    arrays = {
        "x": a["x"], "src": a["src"], "dst": a["dst"], "edge": a["edge_attr_512"],
        "gnn_w": a["L0_gnn_W"], "gnn_b": a["L0_gnn_b"], "diff_w": a["L0_gnn_diffusion_weights"],
        "wr": a["L0_ffn_Wr"], "br": a["L0_ffn_br"],
        "wgate": a["L0_ffn_Wgate"].transpose(1, 0, 2).reshape(D, -1), "bgate": a["L0_ffn_bgate"].reshape(-1),
        "w1": a["L0_ffn_W1"].transpose(1, 0, 2).reshape(D, -1), "w3": a["L0_ffn_W3"].transpose(1, 0, 2).reshape(D, -1),
        "w2": a["L0_ffn_W2"].reshape(-1, D), "coef": a["L1_gnn_path_coeffs"], "paths": a["L1_gnn_path_indices"],
        "ctrl": a["L1_ffn_controller"].reshape(D, -1), "f1": a["L1_ffn_f1"].reshape(D, -1), "f2": a["L1_ffn_f2"].reshape(-1, D),
    }
    arrays = {k: np.ascontiguousarray(v) for k, v in arrays.items()}
    nc = bacc.Bacc("TRN2", target_bir_lowering=False, num_devices=1)
    args = [nc.dram_tensor(f"in_{k}", v.shape, mybir.dt.from_np(v.dtype), kind="ExternalInput").ap()
            for k, v in arrays.items()]
    out = nc.dram_tensor("out", a["x"].shape, mybir.dt.float32, kind="ExternalOutput").ap()
    graph_and_experts(nc, *args, out)
    r = run_bass_kernel_spmd(nc, [{f"in_{k}": v for k, v in arrays.items()}], core_ids=[0])
    return r.results[0]["out"]
```

```python
import concourse.bass as bass
from concourse import mybir
from contextlib import ExitStack


def graph_and_experts(nc, x, src, dst, edge, gnn_w, gnn_b, diff_w, wr, br, wgate, bgate,
                      w1, w3, w2, coef, paths, ctrl, f1, f2, out):
    F32, BF16, I32 = mybir.dt.float32, mybir.dt.bfloat16, mybir.dt.int32
    ALU, ACT, AX = mybir.AluOpType, mybir.ActivationFunctionType, mybir.AxisListType

    P = 128
    N, D = x.shape
    H = N // P
    KC = D // P
    E = src.shape[0]
    T = E // P
    NP = coef.shape[0]
    U = 32
    NS = D // U
    G = wr.shape[1]
    EX = wgate.shape[1]
    HC = w2.shape[0] // P
    STEPS = diff_w.shape[0] - 1
    TG = 16
    NG = N // TG
    ES = ctrl.shape[1]
    FC = f2.shape[0] // P
    EQ = ES // FC
    FE = P // EQ
    PH = P // TG

    BLOCKS = [11, 12, 11]
    FIRST = [0, 11, 23]
    PT = 4
    SB = (NS * U).bit_length() - 1
    PG = 16
    NB = len(BLOCKS)
    BMAX = max(BLOCKS)
    LATE = FIRST[2]
    SLOTS = 8
    DR = 2
    assert sum(BLOCKS) == T

    with ExitStack() as ctx:
        def sb(name, shape, dt=F32):
            return ctx.enter_context(nc.sbuf_tensor(name, shape, dt))

        def sem(name):
            return ctx.enter_context(nc.semaphore(name))

        psum = ctx.enter_context(nc.psum_tensor("psum", [P, 8 * 512], F32))
        bank = [psum[:, i * 512:(i + 1) * 512] for i in range(8)]

        def path_sums(k):
            return psum[:, bass.ds(k * PT + 4 * 512, PT * U)]

        xs = sb("xs", [P, H, D])
        xn = sb("xn", [P, H, D])
        edges = sb("edges", [P, T, D])
        src_t = sb("src_t", [P, H, T * P], BF16)
        big = sb("big", [P, 2 * (BLOCKS[0] + BMAX) * D])
        prod = sb("prod", [P, SLOTS, BMAX, U])
        dst_oh = sb("dst_oh", [P, DR, N])
        xparts = sb("xparts", [P, 3, H, D], BF16)
        ident = sb("ident", [P, P])
        iota_b = sb("iota_b", [P, N], BF16)
        node_id = sb("node_id", [P, H])
        zero_b = sb("zero_b", [P, P], BF16)
        coef_b = sb("coef_b", [P, NP])
        path_w = sb("path_w", [1, NP], I32)
        idx_f = sb("idx_f", [P, 2, T])
        stats = sb("stats", [P, H, 6])
        mv = sb("mv", [P, H, 2])
        rstd = sb("rstd", [P, H])
        root = sb("root", [P, H + 1])
        eps = sb("eps", [P, 1])
        small = prod[:].rearrange("p s t u -> p (s t u)")

        def carve(base, dt_size=4):
            at = [0]
            flat = base

            def take(shape, dt=F32):
                n = 1
                for s in shape:
                    n *= s
                words = n if dt != BF16 else (n + 1) // 2
                v = flat[:, at[0]:at[0] + words]
                at[0] += words
                assert at[0] <= flat.shape[1], (at[0], flat.shape)
                if dt != F32:
                    v = v.bitcast(dt)
                names = "abcd"[:len(shape)]
                if len(shape) > 1:
                    v = v.rearrange(f"p ({' '.join(names)}) -> p {' '.join(names)}",
                                    **{c: s for c, s in zip(names, shape)})
                return v
            return take

        take = carve(big[:, :])
        w_sb = take([KC, D])
        w1_sb = take([KC, w1.shape[1]])
        w3_sb = take([KC, w3.shape[1]])
        w2_sb = take([HC, D])
        src_oh = take([T, N], BF16)
        dst_ohb = take([T, N], BF16)
        take = carve(big[:, :])
        x1g = [take([BLOCKS[0], D]), take([BMAX, D])]
        esum = [take([BLOCKS[0], D]), take([BMAX, D])]
        late = edges[:, LATE:T, :].rearrange("p t f -> p (t f)")
        take = carve(late)
        xnT = take([KC, N])
        bias_b = take([D])
        eye = take([H, N])
        adj = take([H, N])
        cur = take([H, D])
        src_bc = [take([512], BF16), take([512], BF16)]
        link_b = take([H, N], BF16)
        rsum = take([H, 1])
        rinv = take([H, 1])
        outacc = xparts[:, 0:2].rearrange("p a h d -> p (a h d)").bitcast(F32).rearrange(
            "p (h d) -> p h d", h=H)
        take = carve(late)
        take([KC, N])
        hT = take([HC, N])
        gate = [take([N]), take([N])]
        twT = take([N])
        spread = take([HC * P])
        idx_i = take([2, T], I32)
        src_b = take([T], BF16)
        ident_b = take([P], BF16)
        dw_b = take([STEPS + 1])
        route_bias = take([G + EX])
        tw_sb = take([H * EX])
        w_cat = take([KC, G + EX])
        path_i = take([NP, 3], I32)[0:1]
        take = carve(edges[:, 0:LATE, :].rearrange("p t f -> p (t f)"))
        f1_sb = take([KC, f1.shape[1]])
        f2_lo = take([6, D])
        ctrl_sb = take([KC, ES])
        f2_hi = carve(late)([FC - 6, D])
        take = carve(big[:, :])
        xnT2 = take([KC, N])
        logit = take([N])
        tie = take([N])
        top = take([NG])
        permT = take([N])
        permT_b = take([N], BF16)
        select = take([FC * P], BF16)
        group_of = take([PH])
        perm_bd = take([H, PH, ES])
        yT = take([KC, ES, NG])
        perm_f = take([FC, N])
        inner = take([FC, NG])
        z = take([FC, N])

        def load_words(engine, words, n):
            regs = [engine.alloc_register(f"{engine.engine.name}_word{i}") for i in range(n, n + PG)]
            engine.load(regs, path_w[0:1, n % NP:n % NP + PG])
            for i, r in enumerate(regs):
                words[n + i] = engine.snap(r, donate=True, min_val=0, max_val=2 ** (3 * SB) - 1)

        def column(words, n, k):
            v = words[n]
            if k:
                v = v // 2 ** (SB * k)
            if k < 2:
                v = v % 2 ** SB
            return nc.s_assert_within(v, 0, (NS - 1) * U,
                                      skip_runtime_bounds_check_because="segment numbers are below the segments")

        def f2_sb(c):
            return f2_lo[:, c, :] if c < 6 else f2_hi[:, c - 6, :]

        x_in, idx_in, w_in, w1_in, w3_in, w2_in = (sem(n) for n in
                                                   ("x_in", "idx_in", "w_in", "w1_in", "w3_in", "w2_in"))
        edge_in = [sem(f"edge_in{b}") for b in range(NB)]
        ctrl_in, f1_in, f2_in, f2b_in, small_in, stored = (sem(n) for n in ("ctrl_in", "f1_in", "f2_in", "f2b_in", "small_in", "stored"))
        bias_in, path_in, packed = sem("bias_in"), sem("path_in"), sem("packed")
        made = sem("made")
        const = sem("const")
        chain = sem("chain")
        var_ready, root_ready = sem("var_ready"), sem("root_ready")
        xn_ready, xnT_ps, xnT_ready = sem("xn_ready"), sem("xnT_ps"), sem("xnT_ready")
        idx_ready, onehot = sem("idx_ready"), sem("onehot")
        h_ps, h_ready = sem("h_ps"), sem("h_ready")
        bc_ps, bc_copied, bc_used = sem("bc_ps"), sem("bc_copied"), sem("bc_used")
        cnt_ps, link_ready, sym_ps, adj_ready = (sem(n) for n in ("cnt_ps", "link_ready", "sym_ps", "adj_ready"))
        diff_ps, cur_ready, cur_used = sem("diff_ps"), sem("cur_ready"), sem("cur_used")
        logit_ps, route_in, exp_done, tw_ready, twT_ps, twT_ready = (
            sem(n) for n in ("logit_ps", "route_in", "exp_done", "tw_ready", "twT_ps", "twT_ready"))
        up_ps, gated, hid, tw_ps, hid_w, down_ps, x2_ready = (
            sem(n) for n in ("up_ps", "gated", "hid", "tw_ps", "hid_w", "down_ps", "x2_ready"))
        part_a, part_r, parts_ready = sem("part_a"), sem("part_r"), sem("parts_ready")
        gat_ps, gathered = sem("gat_ps"), sem("gathered")
        cleared, mults, sums, psums = sem("cleared"), sem("mults"), sem("sums"), sem("psums")
        block_ps, block_out = sem("block_ps"), sem("block_out")
        dst_made, scattered, x3_ready = sem("dst_made"), sem("scattered"), sem("x3_ready")
        lg_ps, perm_ready, pt_ps, bd_ready, y_ps, y_even = (
            sem(n) for n in ("lg_ps", "perm_ready", "pt_ps", "bd_ready", "y_ps", "y_even"))
        y_odd = sem("y_odd")
        pf_ps, pf_ready, in_ps, in_ready, z_ready, res_ps, fin = (
            sem(n) for n in ("pf_ps", "pf_ready", "in_ps", "in_ready", "z_ready", "res_ps", "fin"))
        sel_ready = sem("sel_ready")

        block = ctx.enter_context(nc.Block())

        def halves(ap):
            return ap.rearrange("(h p) f -> p h f", p=P)

        def rows(ap):
            return ap.rearrange("(c p) n -> p c n", p=P)

        edge_v = edge.rearrange("(p t) f -> p t f", p=P)

        @block.sync
        def _(sp):
            sp.dma_start(idx_i[:, 0], src.rearrange("(p t) -> p t", p=P)).then_inc(idx_in, 16)
            sp.dma_start(idx_i[:, 1], dst.rearrange("(p t) -> p t", p=P)).then_inc(idx_in, 16)
            sp.dma_start(xs[:], halves(x)).then_inc(x_in, 16)
            sp.dma_start(bias_b, gnn_b.rearrange("(o n) -> o n", o=1).broadcast_to([P, D])).then_inc(bias_in, 16)
            sp.dma_start(dw_b, diff_w.rearrange("(o n) -> o n", o=1).broadcast_to([P, STEPS + 1])).then_inc(bias_in, 16)
            sp.dma_start(w_sb, rows(gnn_w)).then_inc(w_in, 16)
            sp.dma_start(w1_sb, rows(w1)).then_inc(w1_in, 16)
            sp.dma_start(w3_sb, rows(w3)).then_inc(w3_in, 16)
            sp.dma_start(w2_sb, rows(w2)).then_inc(w2_in, 16)
            for b in range(NB - 1):
                t = FIRST[b]
                sp.dma_start(edges[:, t:t + BLOCKS[b], :], edge_v[:, t:t + BLOCKS[b], :]).then_inc(edge_in[b], 16)
            sp.wait_ge(x2_ready, H)
            sp.dma_start(edges[:, LATE:T, :], edge_v[:, LATE:T, :]).then_inc(edge_in[NB - 1], 16)
            sp.wait_ge(mults, NP * (NB - 1))
            sp.dma_start(ctrl_sb, rows(ctrl)).then_inc(ctrl_in, 16)
            sp.dma_start(f1_sb, rows(f1)).then_inc(f1_in, 16)
            sp.dma_start(f2_lo, rows(f2)[:, 0:6, :]).then_inc(f2_in, 16)
            sp.wait_ge(mults, NP * NB)
            sp.dma_start(f2_hi, rows(f2)[:, 6:FC, :]).then_inc(f2b_in, 16)
            for h in range(H):
                sp.wait_ge(fin, h + 1)
                sp.dma_start(halves(out)[:, h, :], xs[:, h, :]).then_inc(stored, 16)
            sp.wait_ge(stored, 16 * H)

        @block.gpsimd
        def _(pool):
            def eye_of(ap, base, made_at):
                pool.wait_ge(made, made_at)
                return nc.gpsimd.affine_select(out=ap, in_=ap, compare_op=ALU.not_equal, fill=1.0, base=base,
                                               pattern=[[-1, ap.shape[-1]]], channel_multiplier=1)
            nc.gpsimd.memset(ident[:], 0.0).then_inc(made, 1)
            nc.gpsimd.memset(ident_b, 0.0).then_inc(made, 1)
            nc.gpsimd.memset(eye, 0.0).then_inc(made, 1)
            nc.gpsimd.memset(zero_b[:], 0.0).then_inc(const, 1)
            nc.gpsimd.iota(iota_b[:], pattern=[[1, N]], base=0, channel_multiplier=0,
                           allow_small_or_imprecise_dtypes=True).then_inc(const, 1)
            nc.gpsimd.iota(node_id[:], pattern=[[P, H]], base=0, channel_multiplier=1,
                           allow_small_or_imprecise_dtypes=True).then_inc(const, 1)
            nc.gpsimd.memset(eps[:], 1e-5).then_inc(const, 1)
            eye_of(ident[:], 0, 1).then_inc(const, 1)
            eye_of(ident_b, 0, 2).then_inc(const, 1)
            for h in range(H):
                eye_of(eye[:, h, :], P * h, 3).then_inc(const, 1)

            pool.wait_ge(xn_ready, 2 * H)
            nc.gpsimd.memset(spread[0:EX, :], 0.0).then_inc(made, 1)
            pool.wait_ge(made, 4)
            sp_v = spread[0:EX, :].rearrange("k (e j) -> k e j", e=EX)
            nc.gpsimd.affine_select(out=sp_v, in_=sp_v, compare_op=ALU.not_equal, fill=1.0, base=0,
                                    pattern=[[-1, EX], [0, HC * P // EX]], channel_multiplier=1).then_inc(sel_ready, 1)

            def clear(b):
                if b == 0:
                    pool.wait_ge(x2_ready, H)
                if b >= 2:
                    pool.wait_ge(scattered, FIRST[b - 1])
                nc.gpsimd.memset(esum[b % 2][:, PT:BLOCKS[b], :], 0.0).then_inc(cleared, 1)

            clear(0)
            clear(1)
            for b in range(NB):
                for t in range(FIRST[b], FIRST[b] + BLOCKS[b]):
                    if t >= DR:
                        pool.wait_ge(scattered, t - DR + 1)
                    nc.gpsimd.tensor_scalar(dst_oh[:, t % DR, :], iota_b[:], idx_f[:, 1, t:t + 1], None,
                                            ALU.is_equal).then_inc(dst_made, 1)
                if b + 2 < NB:
                    clear(b + 2)

            pool.wait_ge(x3_ready, H)
            nc.gpsimd.memset(select[0:ES, :], 0.0).then_inc(made, 1)
            nc.gpsimd.memset(group_of, 1.0).then_inc(made, 1)
            nc.gpsimd.iota(tie[0:ES, :].rearrange("p (g t) -> p g t", t=TG), pattern=[[0, NG], [1, TG]], base=0,
                           channel_multiplier=0, allow_small_or_imprecise_dtypes=True).then_inc(sel_ready, 1)
            pool.wait_ge(made, 6)
            nc.gpsimd.affine_select(out=group_of, in_=group_of, compare_op=ALU.is_ge, fill=0.0, base=0,
                                    pattern=[[-TG, PH]], channel_multiplier=1).then_inc(made, 1)
            pool.wait_ge(made, 7)
            nc.gpsimd.affine_select(out=group_of, in_=group_of, compare_op=ALU.is_ge, fill=0.0, base=TG - 1,
                                    pattern=[[TG, PH]], channel_multiplier=-1).then_inc(sel_ready, 1)
            se_v = select[0:ES, :].rearrange("k (e j) -> k e j", e=ES)
            nc.gpsimd.affine_select(out=se_v, in_=se_v, compare_op=ALU.not_equal, fill=1.0, base=0,
                                    pattern=[[-1, ES], [0, FE]], channel_multiplier=1).then_inc(sel_ready, 1)

        @block.scalar
        def _(act):
            act.dma_start(route_bias[:, 0:G], br.rearrange("(o n) -> o n", o=1).broadcast_to([P, G])).then_inc(small_in, 16)
            act.dma_start(route_bias[:, G:], bgate.rearrange("(o n) -> o n", o=1).broadcast_to([P, EX])).then_inc(small_in, 16)
            act.dma_start(w_cat[:, :, 0:G], rows(wr)).then_inc(small_in, 16)
            act.dma_start(w_cat[:, :, G:], rows(wgate)).then_inc(small_in, 16)
            act.dma_start(coef_b[:], coef.rearrange("(o n) -> o n", o=1).broadcast_to([P, NP])).then_inc(small_in, 16)
            act.dma_start(path_i, paths.rearrange("(o n) k -> o n k", o=1)).then_inc(path_in, 16)

            def root_of_variance(n, h):
                act.wait_ge(var_ready, H * n + h + 1)
                nc.scalar.activation(root[:, h:h + 1], mv[:, h, 1:2], ACT.Sqrt, bias=eps[:]).then_inc(root_ready, 1)

            def copy_xnT(stage, to):
                act.wait_ge(xnT_ps, 2 * stage + 1)
                nc.scalar.activation(to[:, 0:2, :].rearrange("p c n -> p (c n)"), bank[0], ACT.Copy)\
                    .then_inc(xnT_ready, 1)

            act.wait_ge(const, 4)
            for h in range(H):
                root_of_variance(0, h)
            copy_xnT(0, xnT)
            act.wait_ge(xnT_ps, 2)
            nc.scalar.activation(xnT[:, 2:4, :].rearrange("p c n -> p (c n)"), bank[1], ACT.Copy).then_inc(xnT_ready, 1)
            for q in range(-(-T // 4)):
                n = min(4, T - 4 * q) * P
                act.wait_ge(bc_ps, q + 1)
                if q >= 2:
                    act.wait_ge(bc_used, q - 1)
                nc.scalar.activation(src_bc[q % 2][:, 0:n], bank[6 + q % 2][:, 0:n], ACT.Copy).then_inc(bc_copied, 1)
            act.wait_ge(adj_ready, 1)
            for s in range(STEPS):
                act.wait_ge(diff_ps, H * (s + 1))
                act.wait_ge(cur_used, H * (s + 1))
                for h in range(H):
                    nc.scalar.activation(cur[:, h, :], bank[(4, 2)[s % 2] + h], ACT.Copy,
                                         scale=rinv[:, h, :]).then_inc(cur_ready, 1)

            for h in range(H):
                root_of_variance(1, h)
            copy_xnT(1, xnT)
            act.wait_ge(route_in, 1)
            nc.scalar.activation(small[:, 0:40], small[:, 0:40], ACT.Exp).then_inc(exp_done, 1)
            for c in range(HC):
                act.wait_ge(up_ps, c + 1)
                if c >= 2:
                    act.wait_ge(hid, c - 1)
                nc.scalar.activation(gate[c % 2], bank[2 + c % 4][:, 0:N], ACT.Silu).then_inc(gated, 1)

            nc.scalar.activation(root[:, H:H + 1], eps[:], ACT.Sqrt)
            for h in range(H):
                root_of_variance(2, h)
                act.wait_ge(xn_ready, 2 * H + h + 1)
                nc.scalar.activation(xparts[:, 0, h, :], xn[:, h, :], ACT.Copy).then_inc(part_a, 1)
            for k in (1, 2):
                for h in range(H):
                    act.wait_ge(part_r, H * (k - 1) + h + 1)
                    nc.scalar.activation(xparts[:, k, h, :], xn[:, h, :], ACT.Copy).then_inc(part_a, 1)

            def copy_gathered(b):
                for t in range(FIRST[b], FIRST[b] + BLOCKS[b]):
                    act.wait_ge(gat_ps, t + 1)
                    if b >= 2 and t == FIRST[b]:
                        act.wait_ge(mults, NP * (b - 1))
                    nc.scalar.activation(x1g[b % 2][:, t - FIRST[b], :], bank[t % 2], ACT.Copy).then_inc(gathered, 1)

            copy_gathered(0)
            for b in range(NB):
                if b + 1 < NB:
                    copy_gathered(b + 1)
                if b >= 2:
                    act.wait_ge(scattered, FIRST[b - 1])
                for q in range(4):
                    act.wait_ge(block_ps, 4 * b + q + 1)
                    nc.scalar.activation(
                        esum[b % 2][:, 0:PT, q * P:(q + 1) * P].rearrange("p t (k u) -> p k t u", u=U),
                        bank[4 + q].rearrange("p (k t u) -> p k t u", t=PT, u=U), ACT.Copy).then_inc(block_out, 1)

            for h in range(H):
                root_of_variance(3, h)
            copy_xnT(2, xnT2)
            for j in range(FC // 2):
                act.wait_ge(pf_ps, j + 1)
                nc.scalar.activation(perm_f[:, 2 * j:2 * j + 2, :].rearrange("p c n -> p (c n)"), bank[6 + j % 2],
                                     ACT.Copy).then_inc(pf_ready, 1)
            for i in range(0, 2 * KC, 2):
                act.wait_ge(y_ps, i + 1)
                nc.scalar.activation(yT[:, i // 2, :, 0:PH].rearrange("p e g -> p g e"),
                                     bank[i % 4].rearrange("p (g e) -> p g e", e=ES), ACT.Copy).then_inc(y_even, 1)
            act.wait_ge(in_ps, 1)
            for q in range(2):
                for k in range(2):
                    nc.scalar.activation(
                        inner[FE * q:FE * (q + 1), 8 * k:8 * k + 8, :],
                        bank[4 + k][FE * q:FE * (q + 1), :].rearrange("p (c e g) -> p c e g", e=EQ, g=NG)[:, :, q, :],
                        ACT.Relu).then_inc(in_ready, 1)

        @block.vector
        def _(dve):
            links = [0]
            lns = [0]

            def link(ins):
                links[0] += 1
                ins.then_inc(chain, 1)
                dve.wait_ge(chain, links[0])

            def variance(h):
                link(nc.vector.bn_stats(out=stats[:, h, :], in_=xs[:, h, :]))
                nc.vector.bn_aggr(out=mv[:, h, :], in_=stats[:, h, :]).then_inc(var_ready, 1)

            def normalise(h):
                lns[0] += 1
                dve.wait_ge(root_ready, lns[0])
                link(nc.vector.reciprocal(rstd[:, h:h + 1], root[:, h:h + 1]))
                nc.vector.tensor_scalar(xn[:, h, :], xs[:, h, :], mv[:, h, 0:1], rstd[:, h:h + 1],
                                        ALU.subtract, ALU.mult).then_inc(xn_ready, 1)

            def copy_xnT(stage, to):
                dve.wait_ge(xnT_ps, 2 * stage + 2)
                nc.vector.tensor_copy(to[:, 2:4, :].rearrange("p c n -> p (c n)"), bank[1]).then_inc(xnT_ready, 1)

            def one_hots(lo, hi):
                for t in range(lo, hi):
                    nc.vector.tensor_scalar(src_oh[:, t, :], iota_b[:], idx_f[:, 0, t:t + 1], None, ALU.is_equal)\
                        .then_inc(onehot, 1)
                    nc.vector.tensor_scalar(dst_ohb[:, t, :], iota_b[:], idx_f[:, 1, t:t + 1], None, ALU.is_equal)\
                        .then_inc(onehot, 1)

            dve.wait_ge(idx_in, 32)
            nc.vector.tensor_copy(idx_f[:], idx_i).then_inc(idx_ready, 1)
            nc.vector.tensor_copy(src_b, idx_i[:, 0]).then_inc(idx_ready, 1)
            dve.wait_ge(x_in, 16)
            for h in range(H):
                variance(h)
            dve.wait_ge(idx_ready, 2)
            dve.wait_ge(const, 3)
            one_hots(0, T // 4)
            for h in range(H):
                normalise(h)
            one_hots(T // 4, T)
            dve.wait_ge(path_in, 16)
            pw = path_w[:].rearrange("o (n k) -> o n k", k=1)
            link(nc.vector.scalar_tensor_tensor(out=pw, in0=path_i[:, :, 2:3], scalar=float(NS * U), in1=path_i[:, :, 1:2],
                                                op0=ALU.mult, op1=ALU.add))
            link(nc.vector.scalar_tensor_tensor(out=pw, in0=pw, scalar=float(NS * U), in1=path_i[:, :, 0:1],
                                                op0=ALU.mult, op1=ALU.add))
            nc.vector.tensor_scalar(pw, pw, float(U), None, ALU.mult).then_inc(packed, 1)
            dve.wait_ge(bias_in, 32)
            for h in range(H):
                dve.wait_ge(h_ps, h + 1)
                nc.vector.tensor_tensor(cur[:, h, :], bank[2 + h], bias_b, ALU.add).then_inc(h_ready, 1)
            for q in range(-(-T // 4)):
                n = min(4, T - 4 * q) * P
                dve.wait_ge(bc_copied, q + 1)
                for h in range(H):
                    last = nc.vector.tensor_scalar(src_t[:, h, q * 512:q * 512 + n], src_bc[q % 2][:, 0:n],
                                                   node_id[:, h:h + 1], None, ALU.is_equal)
                    if h == 0:
                        link(last)
                last.then_inc(bc_used, 1)
            for h in range(H):
                dve.wait_ge(cnt_ps, 1)
                nc.vector.tensor_scalar(link_b[:, h, :], bank[4 + h][:, 0:N], 0.5, None, ALU.is_gt).then_inc(link_ready, 1)
            dve.wait_ge(sym_ps, 1)
            for h in range(H):
                link(nc.vector.scalar_tensor_tensor(out=adj[:, h, :], in0=bank[6][:, h * N:(h + 1) * N], scalar=0.5,
                                                    in1=eye[:, h, :], op0=ALU.is_gt, op1=ALU.add,
                                                    accum_out=rsum[:, h, :]))
            link(nc.vector.tensor_scalar(rsum, rsum, 1.0, None, ALU.max))
            nc.vector.reciprocal(rinv, rsum).then_inc(adj_ready, 1)
            dve.wait_ge(h_ready, H)
            for h in range(H):
                nc.vector.tensor_scalar(outacc[:, h, :], cur[:, h, :], dw_b[:, 0:1], None, ALU.mult).then_inc(cur_used, 1)
            for s in range(STEPS):
                for h in range(H):
                    dve.wait_ge(cur_ready, H * s + h + 1)
                    dve.wait_ge(cur_used, H * s + h + 1)
                    nc.vector.scalar_tensor_tensor(out=outacc[:, h, :], in0=cur[:, h, :], scalar=dw_b[:, s + 1:s + 2],
                                                   in1=outacc[:, h, :], op0=ALU.mult, op1=ALU.add).then_inc(cur_used, 1)
            for h in range(H):
                dve.wait_ge(cur_used, H * STEPS + h + 1)
                link(nc.vector.scalar_tensor_tensor(out=xs[:, h, :], in0=outacc[:, h, :], scalar=0.0,
                                                    in1=xs[:, h, :], op0=ALU.max, op1=ALU.add))
                variance(h)

            for h in range(H):
                normalise(h)
            copy_xnT(1, xnT)
            dve.wait_ge(small_in, 16 * 5)
            R = H * (1 + G)
            sm = [0]

            def room(n):
                v = small[:, sm[0]:sm[0] + n]
                sm[0] += n
                return v
            prob = room(R * G)
            p2 = prob.rearrange("p (r k) -> p r k", k=G)
            dve.wait_ge(logit_ps, 1)
            link(nc.vector.tensor_tensor(prob.rearrange("p (h k) -> p h k", h=H),
                                         bank[6][:, 0:R * G].rearrange("p (h k) -> p h k", h=H),
                                         route_bias.rearrange("p (o k) -> p o k", o=1).broadcast_to([P, H, G + EX]), ALU.add))
            mx = room(R).rearrange("p (r o) -> p r o", o=1)
            link(nc.vector.tensor_reduce(mx, p2, AX.X, ALU.max))
            nc.vector.tensor_tensor(p2, p2, mx.broadcast_to([P, R, G]), ALU.subtract).then_inc(route_in, 1)
            dve.wait_ge(exp_done, 1)
            link(nc.vector.tensor_reduce(mx, p2, AX.X, ALU.add))
            link(nc.vector.reciprocal(mx, mx))
            link(nc.vector.tensor_tensor(p2, p2, mx.broadcast_to([P, R, G]), ALU.mult))
            def pairs():
                return room(R * G * G).rearrange("p (r i j) -> p r i j", i=G, j=G)
            gt, eq = pairs(), pairs()
            low = room(G * G).rearrange("p (i j) -> p i j", j=G)
            for i in range(G):
                for j in range(G):
                    last = nc.vector.memset(low[:, i, j:j + 1], 1.0 if j < i else 0.0)
            link(last)
            pj = p2.rearrange("p r (o k) -> p r o k", o=1).broadcast_to([P, R, G, G])
            pi = p2.rearrange("p r (k o) -> p r k o", o=1).broadcast_to([P, R, G, G])
            link(nc.vector.tensor_tensor(gt, pj, pi, ALU.is_gt))
            link(nc.vector.tensor_tensor(eq, pj, pi, ALU.is_equal))
            link(nc.vector.tensor_tensor(
                eq.rearrange("p r i j -> p r (i j)"), eq.rearrange("p r i j -> p r (i j)"),
                low.rearrange("p (o i) j -> p o (i j)", o=1).broadcast_to([P, R, G * G]), ALU.mult))
            link(nc.vector.tensor_tensor(gt, gt, eq, ALU.add))
            rank = room(R * G).rearrange("p (r k) -> p r k", k=G)
            link(nc.vector.tensor_reduce(rank.rearrange("p r (k o) -> p r k o", o=1), gt, AX.X, ALU.add))
            first, second = (room(R * G).rearrange("p (r k) -> p r k", k=G) for _ in range(2))
            s1, s2, keep = (room(R).rearrange("p (r o) -> p r o", o=1) for _ in range(3))
            link(nc.vector.scalar_tensor_tensor(out=first, in0=rank, scalar=0.0, in1=p2, op0=ALU.is_equal, op1=ALU.mult))
            link(nc.vector.scalar_tensor_tensor(out=second, in0=rank, scalar=1.0, in1=p2, op0=ALU.is_equal, op1=ALU.mult))
            link(nc.vector.tensor_reduce(s1, first, AX.X, ALU.add))
            link(nc.vector.tensor_reduce(s2, second, AX.X, ALU.add))
            link(nc.vector.tensor_tensor(keep, s1, s2, ALU.add))
            link(nc.vector.tensor_scalar(keep, keep, 0.9, None, ALU.is_le))
            link(nc.vector.tensor_tensor(s2, s2, keep, ALU.mult))
            link(nc.vector.tensor_tensor(second, second, keep.broadcast_to([P, R, G]), ALU.mult))
            link(nc.vector.tensor_tensor(first, first, second, ALU.add))
            link(nc.vector.scalar_tensor_tensor(out=s1, in0=s1, scalar=1e-9, in1=s2, op0=ALU.add, op1=ALU.add))
            link(nc.vector.reciprocal(s1, s1))
            link(nc.vector.tensor_tensor(first, first, s1.broadcast_to([P, R, G]), ALU.mult))
            tw = tw_sb.rearrange("p (h g k) -> p h g k", h=H, g=G)
            fh = first.rearrange("p (h r) k -> p h r k", h=H)
            for h in range(H):
                nc.vector.scalar_tensor_tensor(
                    out=tw[:, h], in0=fh[:, h, 0, :].rearrange("p (k o) -> p k o", o=1).broadcast_to([P, G, G]),
                    scalar=float(G) ** -0.5, in1=fh[:, h, 1:, :], op0=ALU.mult, op1=ALU.mult).then_inc(tw_ready, 1)

            def hidden(c):
                dve.wait_ge(gated, c + 1)
                nc.vector.tensor_tensor(hT[:, c, :], gate[c % 2], bank[2 + c % 4][:, N:2 * N], ALU.mult).then_inc(hid, 1)

            dve.wait_ge(twT_ps, 1)
            nc.vector.tensor_copy(twT[0:EX, :], bank[7][0:EX, 0:N]).then_inc(twT_ready, 1)
            for c in range(HC):
                hidden(c)
            for j in range(HC // 2):
                dve.wait_ge(tw_ps, j + 1)
                dve.wait_ge(hid, 2 * j + 2)
                v = hT[:, 2 * j:2 * j + 2, :].rearrange("p c n -> p (c n)")
                nc.vector.tensor_tensor(v, v, bank[(0, 1, 6, 7)[j]], ALU.mult).then_inc(hid_w, 1)
            for h in range(H):
                dve.wait_ge(down_ps, h + 1)
                nc.vector.tensor_tensor(xs[:, h, :], xs[:, h, :], bank[2 + h], ALU.add).then_inc(x2_ready, 1)
                dve.wait_ge(x2_ready, h + 1)
                variance(h)
                normalise(h)

            for k in range(2):
                for h in range(H):
                    dve.wait_ge(part_a, H * k + h + 1)
                    dve.wait_ge(xn_ready, 3 * H)
                    if k:
                        dve.wait_ge(part_r, h + 1)
                    nc.vector.tensor_tensor(xn[:, h, :], xn[:, h, :], xparts[:, k, h, :], ALU.subtract).then_inc(part_r, 1)

            nc.vector.memset(prod[:, :, 0:1, 0:1], 0.0).then_inc(sums, SLOTS)
            words = {}
            load_words(dve, words, 0)
            for b in range(NB):
                tiles, p0 = BLOCKS[b], NP * b
                xg, es = x1g[b % 2], esum[b % 2]
                dve.wait_ge(gathered, FIRST[b] + tiles)
                dve.wait_ge(edge_in[b], 16)
                dve.wait_ge(cleared, b + 1)

                def multiply(p):
                    i1, i2 = column(words, p0 + p, 0), column(words, p0 + p, 1)
                    dve.wait_ge(sums, p0 + p + 1)
                    dve.wait_ge(psums, p0 + p + 1)
                    nc.vector.scalar_tensor_tensor(
                        out=prod[:, p % SLOTS, 0:tiles], in0=xg[:, 0:tiles, bass.ds(i1, U)], scalar=coef_b[:, p:p + 1],
                        in1=edges[:, FIRST[b]:FIRST[b] + tiles, bass.ds(i2, U)],
                        op0=ALU.mult, op1=ALU.mult).then_inc(mults, 1)

                def add(p):
                    to = column(words, p0 + p, 2)
                    dve.wait_ge(mults, p0 + p + 1)
                    dve.wait_ge(sums, p0 + p + SLOTS)
                    v = es[:, PT:tiles, bass.ds(to, U)]
                    nc.vector.tensor_tensor(v, v, prod[:, p % SLOTS, PT:tiles], ALU.add).then_inc(sums, 1)

                multiply(0)
                for p in range(NP):
                    if p + 1 < NP:
                        multiply(p + 1)
                    if p % PG == 4 and (b, p) < (NB - 1, NP - PG):
                        load_words(dve, words, p0 + (p // PG + 1) * PG)
                    add(p)
            for h in range(H):
                dve.wait_ge(scattered, T)
                nc.vector.tensor_tensor(xs[:, h, :], xs[:, h, :], bank[2 + h], ALU.add).then_inc(x3_ready, 1)

            for h in range(H):
                dve.wait_ge(x3_ready, h + 1)
                variance(h)
            for h in range(H):
                normalise(h)
            copy_xnT(2, xnT2)
            dve.wait_ge(sel_ready, 4)
            dve.wait_ge(lg_ps, 1)
            link(nc.vector.scalar_tensor_tensor(out=logit[0:ES, :], in0=tie[0:ES, :], scalar=1e-6 / (TG - 1),
                                                in1=bank[4][0:ES, 0:N], op0=ALU.mult, op1=ALU.add))
            lg = logit[0:ES, :].rearrange("p (g t) -> p g t", t=TG)
            tp = top[0:ES, :].rearrange("p (g o) -> p g o", o=1)
            link(nc.vector.tensor_reduce(tp, lg, AX.X, ALU.max))
            link(nc.vector.tensor_tensor(permT[0:ES, :].rearrange("p (g t) -> p g t", t=TG), lg,
                                         tp.broadcast_to([ES, NG, TG]), ALU.is_equal))
            nc.vector.tensor_copy(permT_b[0:ES, :], permT[0:ES, :]).then_inc(perm_ready, 1)
            for h in range(H):
                dve.wait_ge(pt_ps, H)
                nc.vector.tensor_tensor(
                    perm_bd[:, h], bank[5][:, h * ES:(h + 1) * ES].rearrange("p (o e) -> p o e", o=1).broadcast_to([P, PH, ES]),
                    group_of.rearrange("p (g o) -> p g o", o=1).broadcast_to([P, PH, ES]), ALU.mult).then_inc(bd_ready, 1)
            for i in range(1, 2 * KC, 2):
                dve.wait_ge(y_ps, i + 1)
                nc.vector.tensor_copy(yT[:, i // 2, :, PH:].rearrange("p e g -> p g e"),
                                      bank[i % 4].rearrange("p (g e) -> p g e", e=ES)).then_inc(y_odd, 1)
            dve.wait_ge(in_ps, 1)
            for q in range(2, EQ):
                for k in range(2):
                    nc.vector.tensor_scalar(
                        inner[FE * q:FE * (q + 1), 8 * k:8 * k + 8, :],
                        bank[4 + k][FE * q:FE * (q + 1), :].rearrange("p (c e g) -> p c e g", e=EQ, g=NG)[:, :, q, :],
                        0.0, None, ALU.max).then_inc(in_ready, 1)
            dve.wait_ge(in_ready, 8)
            dve.wait_ge(pf_ready, FC // 2)
            for j in range(FC // 2):
                nc.vector.tensor_tensor(
                    z[:, 2 * j:2 * j + 2, :].rearrange("p c (g t) -> p (c g) t", t=TG),
                    perm_f[:, 2 * j:2 * j + 2, :].rearrange("p c (g t) -> p (c g) t", t=TG),
                    inner[:, 2 * j:2 * j + 2, :].rearrange("p c (g o) -> p (c g) o", o=1).broadcast_to([P, 2 * NG, TG]),
                    ALU.mult).then_inc(z_ready, 1)
            for h in range(H):
                dve.wait_ge(res_ps, h + 1)
                nc.vector.tensor_tensor(xs[:, h, :], xs[:, h, :], bank[6 + h], ALU.add).then_inc(fin, 1)

        @block.tensor
        def _(pe):
            mm = nc.tensor.matmul

            def transpose_xn(stage):
                pe.wait_ge(xn_ready, H * (stage + 1 if stage < 2 else 4))
                for half in range(2):
                    for kc in (2 * half, 2 * half + 1):
                        for h in range(H):
                            last = nc.tensor.transpose(bank[half][:, (kc % 2) * N + h * P:(kc % 2) * N + (h + 1) * P],
                                                       xn[:, h, kc * P:(kc + 1) * P], ident[:])
                    last.then_inc(xnT_ps, 1)
                pe.wait_ge(xnT_ready, 2 * (stage + 1))

            pe.wait_ge(const, 4 + 2 + H)
            transpose_xn(0)
            pe.wait_ge(w_in, 16)
            for h in range(H):
                for kc in range(KC):
                    last = mm(bank[2 + h], xnT[:, kc, h * P:(h + 1) * P], w_sb[:, kc, :], start=kc == 0, stop=kc == KC - 1)
                last.then_inc(h_ps, 1)
            pe.wait_ge(idx_ready, 2)
            for q in range(-(-T // 4)):
                if q >= 2:
                    pe.wait_ge(bc_copied, q - 1)
                for t in range(4 * q, min(4 * q + 4, T)):
                    last = mm(bank[6 + q % 2][:, (t % 4) * P:(t % 4 + 1) * P], src_b[:, t:t + 1].broadcast_to([P, P]),
                              ident_b, start=True, stop=True)
                last.then_inc(bc_ps, 1)
            for t in range(T):
                pe.wait_ge(onehot, 2 * (t + 1))
                for h in range(H):
                    last = mm(bank[4 + h][:, 0:N], src_oh[:, t, h * P:(h + 1) * P], dst_ohb[:, t, :], start=t == 0, stop=t == T - 1)
            last.then_inc(cnt_ps, 1)
            pe.wait_ge(bc_copied, -(-T // 4))
            pe.wait_ge(link_ready, H)
            for h in range(H):
                for c in range(H):
                    o = bank[6][:, h * N + c * P:h * N + (c + 1) * P]
                    mm(o, ident_b, link_b[:, h, c * P:(c + 1) * P], start=True, stop=False)
                    last = mm(o, link_b[:, c, h * P:(h + 1) * P], ident_b, start=False, stop=True)
            last.then_inc(sym_ps, 1)
            pe.wait_ge(adj_ready, 1)
            pe.wait_ge(h_ready, H)
            for s in range(STEPS):
                if s:
                    pe.wait_ge(cur_ready, H * s)
                for h in range(H):
                    for c in range(H):
                        last = mm(bank[(4, 2)[s % 2] + h], adj[:, c, h * P:(h + 1) * P], cur[:, c, :], start=c == 0, stop=c == H - 1)
                    last.then_inc(diff_ps, 1)

            transpose_xn(1)
            pe.wait_ge(small_in, 16 * 5)
            for h in range(H):
                for kc in range(KC):
                    last = mm(bank[6][:, h * (G + EX):(h + 1) * (G + EX)], xnT[:, kc, h * P:(h + 1) * P], w_cat[:, kc, :],
                              start=kc == 0, stop=kc == KC - 1)
            last.then_inc(logit_ps, 1)
            pe.wait_ge(w1_in, 16)
            pe.wait_ge(w3_in, 16)
            for c in range(HC):
                if c >= 4:
                    pe.wait_ge(hid, c - 3)
                for n, w in enumerate((w1_sb, w3_sb)):
                    for kc in range(KC):
                        last = mm(bank[2 + c % 4][:, n * N:(n + 1) * N], w[:, kc, c * P:(c + 1) * P], xnT[:, kc, :],
                                  start=kc == 0, stop=kc == KC - 1)
                last.then_inc(up_ps, 1)
                if c == 3:
                    pe.wait_ge(tw_ready, H)
                    for h in range(H):
                        last = nc.tensor.transpose(bank[7][0:EX, h * P:(h + 1) * P], tw_sb[:, h * EX:(h + 1) * EX], ident[:])
                    last.then_inc(twT_ps, 1)
            pe.wait_ge(twT_ready, 1)
            pe.wait_ge(sel_ready, 1)
            for j in range(HC // 2):
                for c in (2 * j, 2 * j + 1):
                    last = mm(bank[(0, 1, 6, 7)[j]][:, (c % 2) * N:(c % 2 + 1) * N], spread[0:EX, c * P:(c + 1) * P], twT[0:EX, :],
                              start=True, stop=True)
                last.then_inc(tw_ps, 1)
            pe.wait_ge(w2_in, 16)
            for h in range(H):
                for c in range(HC):
                    if h == 0 and c % 2 == 0:
                        pe.wait_ge(hid_w, c // 2 + 1)
                    last = mm(bank[2 + h], hT[:, c, h * P:(h + 1) * P], w2_sb[:, c, :], start=c == 0, stop=c == HC - 1)
                last.then_inc(down_ps, 1)

            def gather(t):
                if t >= 2:
                    pe.wait_ge(gathered, t - 1)
                for h in range(H):
                    for k in range(3):
                        last = mm(bank[t % 2], src_t[:, h, t * P:(t + 1) * P], xparts[:, k, h, :],
                                  start=h == 0 and k == 0, stop=h == H - 1 and k == 2)
                last.then_inc(gat_ps, 1)

            def scatter(b, t):
                pe.wait_ge(dst_made, t + 1)
                for h in range(H):
                    last = mm(bank[2 + h], dst_oh[:, t % DR, h * P:(h + 1) * P], esum[b % 2][:, t - FIRST[b], :],
                              start=t == 0, stop=t == T - 1)
                last.then_inc(scattered, 1)

            pe.wait_ge(part_a, 3 * H)
            pe.wait_ge(x2_ready, H)
            for t in range(BLOCKS[0]):
                gather(t)
            pe.wait_ge(packed, 1)
            words = {}
            load_words(pe, words, 0)
            for b in range(NB):
                gathers = list(range(FIRST[b + 1], FIRST[b + 1] + BLOCKS[b + 1])) if b + 1 < NB else []
                scatters = list(range(FIRST[b - 1], FIRST[b])) if b else []
                if b:
                    pe.wait_ge(block_out, 4 * b)
                    pe.wait_ge(sums, SLOTS + NP * b)
                for q in range(4):
                    last = mm(bank[4 + q], zero_b[:], src_t[:, 0, 0:512], start=True, stop=False)
                    if b == 0:
                        last.then_inc(psums, SLOTS // 4)
                for p in range(NP):
                    to = column(words, NP * b + p, 2)
                    pe.wait_ge(mults, NP * b + p + 1)
                    mm(path_sums(to), ident[:], prod[:, p % SLOTS, 0:PT].rearrange("p t u -> p (t u)"),
                       start=False, stop=False, skip_group_check=True).then_inc(psums, 1)
                    if p % 4 == 1 and scatters:
                        scatter(b - 1, scatters.pop(0))
                    if p % 4 == 3 and gathers:
                        gather(gathers.pop(0))
                    if p % PG == 7 and (b, p) < (NB - 1, NP - PG):
                        load_words(pe, words, NP * b + (p // PG + 1) * PG)
                assert not gathers and not scatters
                for q in range(4):
                    mm(bank[4 + q], zero_b[:], src_t[:, 0, 0:512], start=False, stop=True).then_inc(block_ps, 1)
            pe.wait_ge(block_out, 4 * NB)
            pe.wait_ge(sums, SLOTS + NP * NB)
            for t in range(FIRST[NB - 1], T):
                scatter(NB - 1, t)

            transpose_xn(2)
            pe.wait_ge(ctrl_in, 16)
            for kc in range(KC):
                last = mm(bank[4][0:ES, 0:N], ctrl_sb[:, kc, :], xnT2[:, kc, :], start=kc == 0, stop=kc == KC - 1)
            last.then_inc(lg_ps, 1)
            pe.wait_ge(perm_ready, 1)
            for h in range(H):
                nc.tensor.transpose(bank[5][:, h * ES:(h + 1) * ES], permT[0:ES, h * P:(h + 1) * P], ident[0:ES, 0:ES])\
                    .then_inc(pt_ps, 1)
            for j in range(FC // 2):
                if j >= 2:
                    pe.wait_ge(pf_ready, j - 1)
                for c in (2 * j, 2 * j + 1):
                    last = mm(bank[6 + j % 2][:, (c % 2) * N:(c % 2 + 1) * N], select[0:ES, c * P:(c + 1) * P], permT_b[0:ES, :],
                              start=True, stop=True)
                last.then_inc(pf_ps, 1)
            pe.wait_ge(bd_ready, H)
            for i in range(2 * KC):
                if i >= 4:
                    pe.wait_ge((y_even, y_odd)[i % 2], (i - 4) // 2 + 1)
                mm(bank[i % 4], xn[:, i % 2, (i // 2) * P:(i // 2 + 1) * P], perm_bd[:, i % 2].rearrange("p g e -> p (g e)"),
                   start=True, stop=True).then_inc(y_ps, 1)
            pe.wait_ge(y_even, KC)
            pe.wait_ge(y_odd, KC)
            pe.wait_ge(f1_in, 16)
            for c in range(FC):
                for kc in range(KC):
                    last = mm(bank[4 + c // 8][:, (c % 8) * EQ * NG:(c % 8 + 1) * EQ * NG], f1_sb[:, kc, c * P:(c + 1) * P],
                              yT[:, kc, c * EQ:(c + 1) * EQ, :].rearrange("p e g -> p (e g)"), start=kc == 0, stop=kc == KC - 1)
            last.then_inc(in_ps, 1)
            pe.wait_ge(pf_ready, FC // 2)
            pe.wait_ge(f2_in, 16)
            pe.wait_ge(f2b_in, 16)
            for h in range(H):
                for c in range(FC):
                    if h == 0 and c % 2 == 0:
                        pe.wait_ge(z_ready, c // 2 + 1)
                    last = mm(bank[6 + h], z[:, c, h * P:(h + 1) * P], f2_sb(c), start=c == 0, stop=c == FC - 1)
                last.then_inc(res_ps, 1)


def kernel(**inputs):
    import numpy as np
    import concourse.bacc as bacc
    from concourse.bass_utils import run_bass_kernel_spmd

    a = {k: np.asarray(v) for k, v in inputs.items()}
    E, D, HID = a["L0_ffn_W1"].shape
    arrays = {
        "x": a["x"], "src": a["src"], "dst": a["dst"], "edge": a["edge_attr_512"],
        "gnn_w": a["L0_gnn_W"], "gnn_b": a["L0_gnn_b"], "diff_w": a["L0_gnn_diffusion_weights"],
        "wr": a["L0_ffn_Wr"], "br": a["L0_ffn_br"],
        "wgate": a["L0_ffn_Wgate"].transpose(1, 0, 2).reshape(D, -1), "bgate": a["L0_ffn_bgate"].reshape(-1),
        "w1": a["L0_ffn_W1"].transpose(1, 0, 2).reshape(D, -1), "w3": a["L0_ffn_W3"].transpose(1, 0, 2).reshape(D, -1),
        "w2": a["L0_ffn_W2"].reshape(-1, D), "coef": a["L1_gnn_path_coeffs"], "paths": a["L1_gnn_path_indices"],
        "ctrl": a["L1_ffn_controller"].reshape(D, -1), "f1": a["L1_ffn_f1"].reshape(D, -1), "f2": a["L1_ffn_f2"].reshape(-1, D),
    }
    arrays = {k: np.ascontiguousarray(v) for k, v in arrays.items()}
    nc = bacc.Bacc("TRN2", target_bir_lowering=False, num_devices=1)
    args = [nc.dram_tensor(f"in_{k}", v.shape, mybir.dt.from_np(v.dtype), kind="ExternalInput").ap()
            for k, v in arrays.items()]
    out = nc.dram_tensor("out", a["x"].shape, mybir.dt.float32, kind="ExternalOutput").ap()
    graph_and_experts(nc, *args, out)
    r = run_bass_kernel_spmd(nc, [{f"in_{k}": v for k, v in arrays.items()}], core_ids=[0])
    return r.results[0]["out"]
```

```python
import concourse.bass as bass
from concourse import mybir
from contextlib import ExitStack


def graph_and_experts(nc, x, src, dst, edge, gnn_w, gnn_b, diff_w, wr, br, wgate, bgate,
                      w1, w3, w2, coef, paths, ctrl, f1, f2, out):
    F32, BF16, I32 = mybir.dt.float32, mybir.dt.bfloat16, mybir.dt.int32
    ALU, ACT, AX = mybir.AluOpType, mybir.ActivationFunctionType, mybir.AxisListType

    P = 128
    N, D = x.shape
    H = N // P
    KC = D // P
    E = src.shape[0]
    T = E // P
    NP = coef.shape[0]
    U = 32
    NS = D // U
    G = wr.shape[1]
    EX = wgate.shape[1]
    HC = w2.shape[0] // P
    STEPS = diff_w.shape[0] - 1
    TG = 16
    NG = N // TG
    ES = ctrl.shape[1]
    FC = f2.shape[0] // P
    EQ = ES // FC
    FE = P // EQ
    PH = P // TG

    BLOCKS = [10, 14, 10]
    FIRST = [0, 10, 24]
    KEPT = [5, 5, 4]
    PT = 4
    SB = (NS * U).bit_length() - 1
    PG = 16
    NB = len(BLOCKS)
    QT = -(-T // 4)
    BMAX = max(BLOCKS)
    LATE = FIRST[2]
    SLOTS = 7
    DR = 2
    SPLIT = 5
    assert sum(BLOCKS) == T and STEPS == 3

    with ExitStack() as ctx:
        def sb(name, shape, dt=F32):
            return ctx.enter_context(nc.sbuf_tensor(name, shape, dt))

        def sem(name):
            return ctx.enter_context(nc.semaphore(name))

        psum = ctx.enter_context(nc.psum_tensor("psum", [P, 8 * 512], F32))
        bank = [psum[:, i * 512:(i + 1) * 512] for i in range(8)]

        def path_sums(k):
            return psum[:, bass.ds(k * PT + 4 * 512, PT * U)]

        xs = sb("xs", [P, H, D])
        xn = sb("xn", [P, H, D])
        edges = sb("edges", [P, T, D])
        src_t = sb("src_t", [P, H, T * P], BF16)
        big = sb("big", [P, KC * D + 2 * KC * w1.shape[1] + HC * D + T * N + 2 * T + 3 * NP])
        prod = sb("prod", [P, SLOTS, BMAX, U])
        dst_oh = sb("dst_oh", [P, DR, N])
        xparts = sb("xparts", [P, 3, H, D], BF16)
        ident = sb("ident", [P, P])
        iota_b = sb("iota_b", [P, N], BF16)
        node_id = sb("node_id", [P, H])
        zero_b = sb("zero_b", [P, P], BF16)
        coef_b = sb("coef_b", [P, NP])
        path_w = sb("path_w", [1, NP], I32)
        idx_f = sb("idx_f", [P, 2, T])
        stats = sb("stats", [P, H, 6])
        mv = sb("mv", [P, H, 2])
        rstd = sb("rstd", [P, H])
        root = sb("root", [P, H + 1])
        eps = sb("eps", [P, 1])
        small = prod[:].rearrange("p s t u -> p (s t u)")

        def carve(base, dt_size=4):
            at = [0]
            flat = base

            def take(shape, dt=F32):
                n = 1
                for s in shape:
                    n *= s
                words = n if dt != BF16 else (n + 1) // 2
                v = flat[:, at[0]:at[0] + words]
                at[0] += words
                assert at[0] <= flat.shape[1], (at[0], flat.shape)
                if dt != F32:
                    v = v.bitcast(dt)
                names = "abcd"[:len(shape)]
                if len(shape) > 1:
                    v = v.rearrange(f"p ({' '.join(names)}) -> p {' '.join(names)}",
                                    **{c: s for c, s in zip(names, shape)})
                return v
            return take

        take = carve(big[:, :])
        w_sb = take([KC, D])
        w1_sb = take([KC, w1.shape[1]])
        w3_sb = take([KC, w3.shape[1]])
        w2_sb = take([HC, D])
        src_oh = take([T, N], BF16)
        dst_ohb = take([T, N], BF16)
        idx_i = take([2, T], I32)
        path_i = take([NP, 3], I32)[0:1]
        take = carve(big[:, :])
        x1g = [take([BLOCKS[0], D]), take([BLOCKS[1], D])]
        sum_room = [take([BLOCKS[0], D]), take([BLOCKS[1] - KEPT[1], D])]
        kept_sums = [sum_room[0][:, 0:KEPT[0], :], x1g[1][:, 0:KEPT[1], :], sum_room[0][:, 0:KEPT[2], :]]
        rest_sums = [sum_room[0][:, KEPT[0]:, :], sum_room[1], sum_room[0][:, KEPT[2]:, :]]
        take = carve(x1g[1][:, KEPT[1]:, :].rearrange("p t f -> p (t f)"))
        sum_parts = take([SPLIT, 3, D], BF16)
        dst_split = take([SPLIT, N], BF16)
        late = edges[:, LATE:T, :].rearrange("p t f -> p (t f)")
        take = carve(late)
        xnT = take([KC, N])
        bias_b = take([D])
        eye = take([H, N])
        adj = take([H, N])
        cur = take([H, D])
        cmat = take([H, N])
        link_b = take([H, N], BF16)
        rsum = take([H, 1])
        rinv = take([H, 1])
        w0sum = take([H, 1])
        series, series2 = (xparts[:, k].rearrange("p h d -> p (h d)").bitcast(F32).rearrange("p (h n) -> p h n", h=H)
                           for k in range(2))
        src_bc = carve(small)([T * P], BF16)
        take = carve(late)
        take([KC, N])
        hT = take([HC, N])
        gate = [take([N]), take([N])]
        twT = take([N])
        spread = take([HC * P])
        src_b = take([T], BF16)
        ident_b = take([P], BF16)
        dw_b = take([STEPS + 1])
        route_bias = take([G + EX])
        tw_sb = take([H * EX])
        w_cat = take([KC, G + EX])
        take = carve(edges[:, 0:LATE, :].rearrange("p t f -> p (t f)"))
        f1_sb = take([KC, f1.shape[1]])
        f2_lo = take([6, D])
        ctrl_sb = take([KC, ES])
        f2_hi = carve(late)([FC - 6, D])
        take = carve(big[:, :])
        xnT2 = take([KC, N])
        logit = take([N])
        tie = take([N])
        top = take([NG])
        permT = take([N])
        permT_b = take([N], BF16)
        select = take([FC * P], BF16)
        group_of = take([PH])
        perm_bd = take([H, PH, ES])
        yT = take([KC, ES, NG])
        perm_f = take([FC, N])
        inner = take([FC, NG])
        z = take([FC, N])

        def load_words(engine, words, n):
            regs = [engine.alloc_register(f"{engine.engine.name}_word{i}") for i in range(n, n + PG)]
            engine.load(regs, path_w[0:1, n % NP:n % NP + PG])
            for i, r in enumerate(regs):
                words[n + i] = engine.snap(r, donate=True, min_val=0, max_val=2 ** (3 * SB) - 1)

        def column(words, n, k):
            v = words[n]
            if k:
                v = v // 2 ** (SB * k)
            if k < 2:
                v = v % 2 ** SB
            return nc.s_assert_within(v, 0, (NS - 1) * U,
                                      skip_runtime_bounds_check_because="segment numbers are below the segments")

        def scatter_order(b):
            tiles = [FIRST[b] + i % BLOCKS[b] for i in range(KEPT[b], KEPT[b] + BLOCKS[b])]
            return [(FIRST[b] + i, t) for i, t in enumerate(tiles)]

        def tile_sums(b, t):
            i = t - FIRST[b]
            return kept_sums[b][:, i, :] if i < KEPT[b] else rest_sums[b][:, i - KEPT[b], :]

        split_tiles = [t for _, t in scatter_order(NB - 1)][BLOCKS[NB - 1] - SPLIT:]

        def gather_bank(t):
            return bank[(0, 1, 2, 4, 5, 6, 7, 3)[t % 8]] if t < BLOCKS[0] else bank[0]

        def copied_before(t):
            return (min(t, BLOCKS[0]) + 1) // 2 + max(t - BLOCKS[0], 0)

        def sum_banks(b):
            return [4, 5, 6, 7] + [1] * (KEPT[b] - PT)

        def banks_before(b):
            return sum(len(sum_banks(i)) for i in range(b))

        def perm_bank(j):
            return bank[6 + j % 2] if j < 4 else bank[j - 4]

        def f2_sb(c):
            return f2_lo[:, c, :] if c < 6 else f2_hi[:, c - 6, :]

        x_in, idx_in, w_in, w1_in, w3_in, w2_in = (sem(n) for n in
                                                   ("x_in", "idx_in", "w_in", "w1_in", "w3_in", "w2_in"))
        edge_in = [sem(f"edge_in{b}") for b in range(NB)]
        ctrl_in, f1_in, f2_in, f2b_in, small_in, stored = (sem(n) for n in ("ctrl_in", "f1_in", "f2_in", "f2b_in", "small_in", "stored"))
        bias_in, path_in, packed = sem("bias_in"), sem("path_in"), sem("packed")
        made = sem("made")
        const = sem("const")
        chain = sem("chain")
        var_ready, root_ready = sem("var_ready"), sem("root_ready")
        xn_ready, xnT_ps, xnT_ready = sem("xn_ready"), sem("xnT_ps"), sem("xnT_ready")
        idx_ready, onehot = sem("idx_ready"), sem("onehot")
        h_ps, h_ready = sem("h_ps"), sem("h_ready")
        bc_ps, bc_copied, src_made = sem("bc_ps"), sem("bc_copied"), sem("src_made")
        cnt_ps, link_ready, sym_ps, adj_ready = (sem(n) for n in ("cnt_ps", "link_ready", "sym_ps", "adj_ready"))
        cmat_ready, s2_ps, s3_ps, series_ready, series2_ready = (
            sem(n) for n in ("cmat_ready", "s2_ps", "s3_ps", "series_ready", "series2_ready"))
        diff_ps, relu_done = sem("diff_ps"), sem("relu_done")
        logit_ps, route_in, exp_done, tw_ready, twT_ps, twT_ready = (
            sem(n) for n in ("logit_ps", "route_in", "exp_done", "tw_ready", "twT_ps", "twT_ready"))
        up_ps, gated, hid, tw_ps, hid_w, down_ps, x2_ready = (
            sem(n) for n in ("up_ps", "gated", "hid", "tw_ps", "hid_w", "down_ps", "x2_ready"))
        part_a, part_r = sem("part_a"), sem("part_r")
        gat_ps, gathered, gathered_odd = sem("gat_ps"), sem("gathered"), sem("gathered_odd")
        cleared, mults, sums, psums = sem("cleared"), sem("mults"), sem("sums"), sem("psums")
        block_ps, block_out = sem("block_ps"), sem("block_out")
        dst_made, scattered, x3_ready = sem("dst_made"), sem("scattered"), sem("x3_ready")
        half_done, dst_split_made = sem("half_done"), sem("dst_split_made")
        hi_done, left_done, mid_done, lo_done = (sem(n) for n in ("hi_done", "left_done", "mid_done", "lo_done"))
        lg_ps, perm_ready, pt_ps, bd_ready, y_ps, y_even = (
            sem(n) for n in ("lg_ps", "perm_ready", "pt_ps", "bd_ready", "y_ps", "y_even"))
        y_odd = sem("y_odd")
        pf_ps, pf_ready, in_ps, in_low, in_high, z_ready, res_ps, fin = (
            sem(n) for n in ("pf_ps", "pf_ready", "in_ps", "in_low", "in_high", "z_ready", "res_ps", "fin"))
        sel_ready = sem("sel_ready")

        block = ctx.enter_context(nc.Block())

        def halves(ap):
            return ap.rearrange("(h p) f -> p h f", p=P)

        def rows(ap):
            return ap.rearrange("(c p) n -> p c n", p=P)

        edge_v = edge.rearrange("(p t) f -> p t f", p=P)

        @block.sync
        def _(sp):
            sp.dma_start(idx_i[:, 0], src.rearrange("(p t) -> p t", p=P)).then_inc(idx_in, 16)
            sp.dma_start(idx_i[:, 1], dst.rearrange("(p t) -> p t", p=P)).then_inc(idx_in, 16)
            sp.dma_start(xs[:], halves(x)).then_inc(x_in, 16)
            sp.dma_start(bias_b, gnn_b.rearrange("(o n) -> o n", o=1).broadcast_to([P, D])).then_inc(bias_in, 16)
            sp.dma_start(dw_b, diff_w.rearrange("(o n) -> o n", o=1).broadcast_to([P, STEPS + 1])).then_inc(bias_in, 16)
            sp.dma_start(w_sb, rows(gnn_w)).then_inc(w_in, 16)
            sp.dma_start(w1_sb, rows(w1)).then_inc(w1_in, 16)
            sp.dma_start(w3_sb, rows(w3)).then_inc(w3_in, 16)
            sp.dma_start(w2_sb, rows(w2)).then_inc(w2_in, 16)
            for b in range(NB - 1):
                t = FIRST[b]
                sp.dma_start(edges[:, t:t + BLOCKS[b], :], edge_v[:, t:t + BLOCKS[b], :]).then_inc(edge_in[b], 16)
            sp.wait_ge(x2_ready, H)
            sp.dma_start(edges[:, LATE:T, :], edge_v[:, LATE:T, :]).then_inc(edge_in[NB - 1], 16)
            sp.wait_ge(mults, NP * (NB - 1))
            sp.dma_start(ctrl_sb, rows(ctrl)).then_inc(ctrl_in, 16)
            sp.dma_start(f1_sb, rows(f1)).then_inc(f1_in, 16)
            sp.dma_start(f2_lo, rows(f2)[:, 0:6, :]).then_inc(f2_in, 16)
            sp.wait_ge(mults, NP * NB)
            sp.dma_start(f2_hi, rows(f2)[:, 6:FC, :]).then_inc(f2b_in, 16)
            for h in range(H):
                sp.wait_ge(fin, h + 1)
                sp.dma_start(halves(out)[:, h, :], xs[:, h, :]).then_inc(stored, 16)
            sp.wait_ge(stored, 16 * H)

        @block.gpsimd
        def _(pool):
            def eye_of(ap, base, made_at):
                pool.wait_ge(made, made_at)
                return nc.gpsimd.affine_select(out=ap, in_=ap, compare_op=ALU.not_equal, fill=1.0, base=base,
                                               pattern=[[-1, ap.shape[-1]]], channel_multiplier=1)
            nc.gpsimd.memset(ident[:], 0.0).then_inc(made, 1)
            nc.gpsimd.memset(ident_b, 0.0).then_inc(made, 1)
            nc.gpsimd.memset(eye, 0.0).then_inc(made, 1)
            nc.gpsimd.memset(zero_b[:], 0.0).then_inc(const, 1)
            nc.gpsimd.iota(iota_b[:], pattern=[[1, N]], base=0, channel_multiplier=0,
                           allow_small_or_imprecise_dtypes=True).then_inc(const, 1)
            nc.gpsimd.iota(node_id[:], pattern=[[P, H]], base=0, channel_multiplier=1,
                           allow_small_or_imprecise_dtypes=True).then_inc(const, 1)
            nc.gpsimd.memset(eps[:], 1e-5).then_inc(const, 1)
            eye_of(ident[:], 0, 1).then_inc(const, 1)
            eye_of(ident_b, 0, 2).then_inc(const, 1)
            for h in range(H):
                eye_of(eye[:, h, :], P * h, 3).then_inc(const, 1)

            pool.wait_ge(xn_ready, 2 * H)
            nc.gpsimd.memset(spread[0:EX, :], 0.0).then_inc(made, 1)
            pool.wait_ge(made, 4)
            sp_v = spread[0:EX, :].rearrange("k (e j) -> k e j", e=EX)
            nc.gpsimd.affine_select(out=sp_v, in_=sp_v, compare_op=ALU.not_equal, fill=1.0, base=0,
                                    pattern=[[-1, EX], [0, HC * P // EX]], channel_multiplier=1).then_inc(sel_ready, 1)

            def clear(b):
                if b == 0:
                    pool.wait_ge(x2_ready, H)
                if b >= 2:
                    pool.wait_ge(scattered, FIRST[b - 1])
                nc.gpsimd.memset(rest_sums[b], 0.0).then_inc(cleared, 1)

            clear(0)
            clear(1)
            for b in range(NB):
                if b == NB - 1:
                    pool.wait_ge(mults, NP * (NB - 1))
                    for i, t in enumerate(split_tiles):
                        nc.gpsimd.tensor_scalar(dst_split[:, i, :], iota_b[:], idx_f[:, 1, t:t + 1], None,
                                                ALU.is_equal).then_inc(dst_split_made, 1)
                for n, t in scatter_order(b):
                    if n >= T - SPLIT:
                        break
                    if n >= DR:
                        pool.wait_ge(scattered, n - DR + 1)
                    nc.gpsimd.tensor_scalar(dst_oh[:, n % DR, :], iota_b[:], idx_f[:, 1, t:t + 1], None,
                                            ALU.is_equal).then_inc(dst_made, 1)
                if b + 2 < NB:
                    clear(b + 2)

            pool.wait_ge(x3_ready, H)
            nc.gpsimd.memset(select[0:ES, :], 0.0).then_inc(made, 1)
            nc.gpsimd.memset(group_of, 1.0).then_inc(made, 1)
            nc.gpsimd.iota(tie[0:ES, :].rearrange("p (g t) -> p g t", t=TG), pattern=[[0, NG], [1, TG]], base=0,
                           channel_multiplier=0, allow_small_or_imprecise_dtypes=True).then_inc(sel_ready, 1)
            pool.wait_ge(made, 6)
            nc.gpsimd.affine_select(out=group_of, in_=group_of, compare_op=ALU.is_ge, fill=0.0, base=0,
                                    pattern=[[-TG, PH]], channel_multiplier=1).then_inc(made, 1)
            pool.wait_ge(made, 7)
            nc.gpsimd.affine_select(out=group_of, in_=group_of, compare_op=ALU.is_ge, fill=0.0, base=TG - 1,
                                    pattern=[[TG, PH]], channel_multiplier=-1).then_inc(sel_ready, 1)
            se_v = select[0:ES, :].rearrange("k (e j) -> k e j", e=ES)
            nc.gpsimd.affine_select(out=se_v, in_=se_v, compare_op=ALU.not_equal, fill=1.0, base=0,
                                    pattern=[[-1, ES], [0, FE]], channel_multiplier=1).then_inc(sel_ready, 1)

        @block.scalar
        def _(act):
            act.dma_start(route_bias[:, 0:G], br.rearrange("(o n) -> o n", o=1).broadcast_to([P, G])).then_inc(small_in, 16)
            act.dma_start(route_bias[:, G:], bgate.rearrange("(o n) -> o n", o=1).broadcast_to([P, EX])).then_inc(small_in, 16)
            act.dma_start(w_cat[:, :, 0:G], rows(wr)).then_inc(small_in, 16)
            act.dma_start(w_cat[:, :, G:], rows(wgate)).then_inc(small_in, 16)
            act.dma_start(coef_b[:], coef.rearrange("(o n) -> o n", o=1).broadcast_to([P, NP])).then_inc(small_in, 16)
            act.dma_start(path_i, paths.rearrange("(o n) k -> o n k", o=1)).then_inc(path_in, 16)

            def root_of_variance(n, h):
                act.wait_ge(var_ready, H * n + h + 1)
                nc.scalar.activation(root[:, h:h + 1], mv[:, h, 1:2], ACT.Sqrt, bias=eps[:]).then_inc(root_ready, 1)

            def copy_xnT(stage, to):
                act.wait_ge(xnT_ps, 2 * stage + 1)
                nc.scalar.activation(to[:, 0:2, :].rearrange("p c n -> p (c n)"), bank[0], ACT.Copy)\
                    .then_inc(xnT_ready, 1)

            act.wait_ge(const, 4)
            def copy_broadcast(lo, hi):
                for q in range(lo, hi):
                    n = min(4, T - 4 * q) * P
                    act.wait_ge(bc_ps, q + 1)
                    nc.scalar.activation(src_bc[:, q * 512:q * 512 + n], bank[6 + q % 2][:, 0:n], ACT.Copy)\
                        .then_inc(bc_copied, 1)
            nc.scalar.activation(root[:, H:H + 1], eps[:], ACT.Sqrt)
            copy_broadcast(0, 3)
            for h in range(H):
                root_of_variance(0, h)
            copy_broadcast(3, QT)
            copy_xnT(0, xnT)
            act.wait_ge(xnT_ps, 2)
            nc.scalar.activation(xnT[:, 2:4, :].rearrange("p c n -> p (c n)"), bank[1], ACT.Copy).then_inc(xnT_ready, 1)
            act.wait_ge(xnT_ready, 2)
            for h in range(H):
                act.wait_ge(diff_ps, h + 1)
                nc.scalar.activation(xn[:, h, :], bank[6 + h], ACT.Relu, scale=rinv[:, h, :]).then_inc(relu_done, 1)

            for h in range(H):
                root_of_variance(1, h)
            copy_xnT(1, xnT)
            act.wait_ge(route_in, 1)
            nc.scalar.activation(small[:, 0:40], small[:, 0:40], ACT.Exp).then_inc(exp_done, 1)
            for c in range(HC):
                act.wait_ge(up_ps, c + 1)
                if c >= 2:
                    act.wait_ge(hid, c - 1)
                nc.scalar.activation(gate[c % 2], bank[2 + c % 4][:, 0:N], ACT.Silu).then_inc(gated, 1)

            nc.scalar.activation(root[:, H:H + 1], eps[:], ACT.Sqrt)
            for h in range(H):
                root_of_variance(2, h)
                act.wait_ge(xn_ready, 2 * H + h + 1)
                nc.scalar.activation(xparts[:, 0, h, :], xn[:, h, :], ACT.Copy).then_inc(part_a, 1)
                act.wait_ge(part_r, 2 * h + 1)
                nc.scalar.activation(xparts[:, 1, h, :], xn[:, h, :], ACT.Copy).then_inc(part_a, 1)

            def copy_gathered(b):
                for t in range(FIRST[b], FIRST[b] + BLOCKS[b], 1 if b else 2):
                    act.wait_ge(gat_ps, t + 1)
                    if b >= 2 and t == FIRST[b]:
                        act.wait_ge(mults, NP * (b - 1))
                    nc.scalar.activation(x1g[b % 2][:, t - FIRST[b], :], gather_bank(t), ACT.Copy).then_inc(gathered, 1)

            copy_gathered(0)
            for b in range(NB):
                if b + 1 < NB:
                    copy_gathered(b + 1)
                if b >= 2:
                    act.wait_ge(scattered, FIRST[b - 1])
                for i, q in enumerate(sum_banks(b)):
                    act.wait_ge(block_ps, banks_before(b) + i + 1)
                    if i < PT:
                        nc.scalar.activation(
                            kept_sums[b][:, 0:PT, i * P:(i + 1) * P].rearrange("p t (k u) -> p k t u", u=U),
                            bank[q].rearrange("p (k t u) -> p k t u", t=PT, u=U), ACT.Copy).then_inc(block_out, 1)
                    else:
                        nc.scalar.activation(kept_sums[b][:, i, :], bank[q], ACT.Copy).then_inc(block_out, 1)

            act.wait_ge(sums, NP * NB)
            act.wait_ge(block_out, banks_before(NB))
            for i in range(SPLIT + 1):
                if i < SPLIT:
                    nc.scalar.activation(sum_parts[:, i, 0, :], tile_sums(NB - 1, split_tiles[i]), ACT.Copy).then_inc(hi_done, 1)
                if i:
                    act.wait_ge(left_done, i)
                    nc.scalar.activation(sum_parts[:, i - 1, 1, :], tile_sums(NB - 1, split_tiles[i - 1]), ACT.Copy)\
                        .then_inc(mid_done, 1)

            for h in range(H):
                root_of_variance(3, h)
            copy_xnT(2, xnT2)
            def copy_perm(lo, hi):
                for j in range(lo, hi):
                    act.wait_ge(pf_ps, j + 1)
                    nc.scalar.activation(perm_f[:, 2 * j:2 * j + 2, :].rearrange("p c n -> p (c n)"), perm_bank(j),
                                         ACT.Copy).then_inc(pf_ready, 1)

            copy_perm(0, 2)
            for i in range(0, 2 * KC, 2):
                act.wait_ge(y_ps, i + 1)
                nc.scalar.activation(yT[:, i // 2, :, 0:PH].rearrange("p e g -> p g e"),
                                     bank[i % 4].rearrange("p (g e) -> p g e", e=ES), ACT.Copy).then_inc(y_even, 1)
            copy_perm(2, 4)
            for k in range(2):
                act.wait_ge(in_ps, k + 1)
                for q in range(2):
                    nc.scalar.activation(
                        inner[FE * q:FE * (q + 1), 8 * k:8 * k + 8, :],
                        bank[4 + k][FE * q:FE * (q + 1), :].rearrange("p (c e g) -> p c e g", e=EQ, g=NG)[:, :, q, :],
                        ACT.Relu).then_inc(in_low, 1)
                if k == 0:
                    copy_perm(4, FC // 2)

        @block.vector
        def _(dve):
            links = [0]
            lns = [0]

            def link(ins):
                links[0] += 1
                ins.then_inc(chain, 1)
                dve.wait_ge(chain, links[0])

            def variance(h):
                link(nc.vector.bn_stats(out=stats[:, h, :], in_=xs[:, h, :]))
                nc.vector.bn_aggr(out=mv[:, h, :], in_=stats[:, h, :]).then_inc(var_ready, 1)

            def normalise(h):
                lns[0] += 1
                dve.wait_ge(root_ready, lns[0])
                link(nc.vector.reciprocal(rstd[:, h:h + 1], root[:, h:h + 1]))
                nc.vector.tensor_scalar(xn[:, h, :], xs[:, h, :], mv[:, h, 0:1], rstd[:, h:h + 1],
                                        ALU.subtract, ALU.mult).then_inc(xn_ready, 1)

            def copy_xnT(stage, to):
                dve.wait_ge(xnT_ps, 2 * stage + 2)
                nc.vector.tensor_copy(to[:, 2:4, :].rearrange("p c n -> p (c n)"), bank[1]).then_inc(xnT_ready, 1)

            def one_hots(lo, hi):
                for t in range(lo, hi):
                    nc.vector.tensor_scalar(src_oh[:, t, :], iota_b[:], idx_f[:, 0, t:t + 1], None, ALU.is_equal)\
                        .then_inc(onehot, 1)
                    nc.vector.tensor_scalar(dst_ohb[:, t, :], iota_b[:], idx_f[:, 1, t:t + 1], None, ALU.is_equal)\
                        .then_inc(onehot, 1)

            dve.wait_ge(idx_in, 32)
            nc.vector.tensor_copy(idx_f[:], idx_i).then_inc(idx_ready, 1)
            nc.vector.tensor_copy(src_b, idx_i[:, 0]).then_inc(idx_ready, 1)
            dve.wait_ge(x_in, 16)
            for h in range(H):
                variance(h)
            dve.wait_ge(idx_ready, 2)
            dve.wait_ge(const, 3)
            one_hots(0, T // 4)
            for h in range(H):
                normalise(h)
            one_hots(T // 4, T)
            dve.wait_ge(path_in, 16)
            pw = path_w[:].rearrange("o (n k) -> o n k", k=1)
            link(nc.vector.scalar_tensor_tensor(out=pw, in0=path_i[:, :, 2:3], scalar=float(NS * U), in1=path_i[:, :, 1:2],
                                                op0=ALU.mult, op1=ALU.add))
            link(nc.vector.scalar_tensor_tensor(out=pw, in0=pw, scalar=float(NS * U), in1=path_i[:, :, 0:1],
                                                op0=ALU.mult, op1=ALU.add))
            nc.vector.tensor_scalar(pw, pw, float(U), None, ALU.mult).then_inc(packed, 1)
            for h in range(H):
                dve.wait_ge(cnt_ps, 1)
                nc.vector.tensor_scalar(link_b[:, h, :], bank[4 + h][:, 0:N], 0.5, None, ALU.is_gt).then_inc(link_ready, 1)

            def src_one_hots(lo, hi):
                for q in range(lo, hi):
                    n = min(4, T - 4 * q) * P
                    dve.wait_ge(bc_copied, q + 1)
                    for h in range(H):
                        nc.vector.tensor_scalar(src_t[:, h, q * 512:q * 512 + n], src_bc[:, q * 512:q * 512 + n],
                                                node_id[:, h:h + 1], None, ALU.is_equal).then_inc(src_made, 1)
            dve.wait_ge(bias_in, 32)
            dve.wait_ge(sym_ps, 1)
            for h in range(H):
                last = nc.vector.scalar_tensor_tensor(out=adj[:, h, :], in0=bank[0][:, h * N:(h + 1) * N], scalar=0.5,
                                                      in1=eye[:, h, :], op0=ALU.is_gt, op1=ALU.add,
                                                      accum_out=rsum[:, h, :])
                last.then_inc(adj_ready, 1)
            dve.wait_ge(adj_ready, H)
            link(nc.vector.tensor_scalar(rsum, rsum, 1.0, None, ALU.max))
            link(nc.vector.reciprocal(rinv, rsum))
            for h in range(H):
                nc.vector.tensor_scalar(cmat[:, h, :], adj[:, h, :], rinv[:, h, :], None, ALU.mult).then_inc(cmat_ready, 1)
            nc.vector.tensor_scalar(series2, adj, dw_b[:, 2:3], None, ALU.mult).then_inc(chain, 1)
            nc.vector.tensor_scalar(series, adj, dw_b[:, 1:2], None, ALU.mult).then_inc(chain, 1)
            nc.vector.tensor_scalar(w0sum, rsum, dw_b[:, 0:1], None, ALU.mult).then_inc(chain, 1)
            links[0] += 3
            dve.wait_ge(chain, links[0])
            for h in range(H):
                link(nc.vector.scalar_tensor_tensor(out=series[:, h, :], in0=eye[:, h, :], scalar=w0sum[:, h, :],
                                                    in1=series[:, h, :], op0=ALU.mult, op1=ALU.add))
            src_one_hots(0, 1)
            dve.wait_ge(h_ps, 1)
            nc.vector.tensor_tensor(cur[:, 0, :], bank[2], bias_b, ALU.add).then_inc(h_ready, 1)
            dve.wait_ge(s2_ps, 1)
            for h in range(H):
                nc.vector.scalar_tensor_tensor(out=series2[:, h, :], in0=bank[1][:, h * N:(h + 1) * N], scalar=dw_b[:, 3:4],
                                               in1=series2[:, h, :], op0=ALU.mult, op1=ALU.add).then_inc(series2_ready, 1)
            dve.wait_ge(h_ps, 2)
            nc.vector.tensor_tensor(cur[:, 1, :], bank[3], bias_b, ALU.add).then_inc(h_ready, 1)
            src_one_hots(1, 3)
            dve.wait_ge(s3_ps, 1)
            for h in range(H):
                nc.vector.tensor_tensor(series[:, h, :], series[:, h, :], bank[4][:, h * N:(h + 1) * N], ALU.add)\
                    .then_inc(series_ready, 1)
            src_one_hots(3, QT)
            for h in range(H):
                dve.wait_ge(relu_done, h + 1)
                link(nc.vector.tensor_tensor(xs[:, h, :], xs[:, h, :], xn[:, h, :], ALU.add))
                variance(h)

            for h in range(H):
                normalise(h)
            copy_xnT(1, xnT)
            dve.wait_ge(small_in, 16 * 5)
            R = H * (1 + G)
            sm = [0]

            def room(n):
                v = small[:, sm[0]:sm[0] + n]
                sm[0] += n
                return v
            prob = room(R * G)
            p2 = prob.rearrange("p (r k) -> p r k", k=G)
            dve.wait_ge(logit_ps, 1)
            link(nc.vector.tensor_tensor(prob.rearrange("p (h k) -> p h k", h=H),
                                         bank[6][:, 0:R * G].rearrange("p (h k) -> p h k", h=H),
                                         route_bias.rearrange("p (o k) -> p o k", o=1).broadcast_to([P, H, G + EX]), ALU.add))
            mx = room(R).rearrange("p (r o) -> p r o", o=1)
            link(nc.vector.tensor_reduce(mx, p2, AX.X, ALU.max))
            nc.vector.tensor_tensor(p2, p2, mx.broadcast_to([P, R, G]), ALU.subtract).then_inc(route_in, 1)
            dve.wait_ge(exp_done, 1)
            link(nc.vector.tensor_reduce(mx, p2, AX.X, ALU.add))
            link(nc.vector.reciprocal(mx, mx))
            link(nc.vector.tensor_tensor(p2, p2, mx.broadcast_to([P, R, G]), ALU.mult))
            def pairs():
                return room(R * G * G).rearrange("p (r i j) -> p r i j", i=G, j=G)
            gt, eq = pairs(), pairs()
            low = room(G * G).rearrange("p (i j) -> p i j", j=G)
            for i in range(G):
                for j in range(G):
                    last = nc.vector.memset(low[:, i, j:j + 1], 1.0 if j < i else 0.0)
            link(last)
            pj = p2.rearrange("p r (o k) -> p r o k", o=1).broadcast_to([P, R, G, G])
            pi = p2.rearrange("p r (k o) -> p r k o", o=1).broadcast_to([P, R, G, G])
            link(nc.vector.tensor_tensor(gt, pj, pi, ALU.is_gt))
            link(nc.vector.tensor_tensor(eq, pj, pi, ALU.is_equal))
            link(nc.vector.tensor_tensor(
                eq.rearrange("p r i j -> p r (i j)"), eq.rearrange("p r i j -> p r (i j)"),
                low.rearrange("p (o i) j -> p o (i j)", o=1).broadcast_to([P, R, G * G]), ALU.mult))
            link(nc.vector.tensor_tensor(gt, gt, eq, ALU.add))
            rank = room(R * G).rearrange("p (r k) -> p r k", k=G)
            link(nc.vector.tensor_reduce(rank.rearrange("p r (k o) -> p r k o", o=1), gt, AX.X, ALU.add))
            first, second = (room(R * G).rearrange("p (r k) -> p r k", k=G) for _ in range(2))
            s1, s2, keep = (room(R).rearrange("p (r o) -> p r o", o=1) for _ in range(3))
            link(nc.vector.scalar_tensor_tensor(out=first, in0=rank, scalar=0.0, in1=p2, op0=ALU.is_equal, op1=ALU.mult))
            link(nc.vector.scalar_tensor_tensor(out=second, in0=rank, scalar=1.0, in1=p2, op0=ALU.is_equal, op1=ALU.mult))
            link(nc.vector.tensor_reduce(s1, first, AX.X, ALU.add))
            link(nc.vector.tensor_reduce(s2, second, AX.X, ALU.add))
            link(nc.vector.tensor_tensor(keep, s1, s2, ALU.add))
            link(nc.vector.tensor_scalar(keep, keep, 0.9, None, ALU.is_le))
            link(nc.vector.tensor_tensor(s2, s2, keep, ALU.mult))
            link(nc.vector.tensor_tensor(second, second, keep.broadcast_to([P, R, G]), ALU.mult))
            link(nc.vector.tensor_tensor(first, first, second, ALU.add))
            link(nc.vector.scalar_tensor_tensor(out=s1, in0=s1, scalar=1e-9, in1=s2, op0=ALU.add, op1=ALU.add))
            link(nc.vector.reciprocal(s1, s1))
            link(nc.vector.tensor_tensor(first, first, s1.broadcast_to([P, R, G]), ALU.mult))
            tw = tw_sb.rearrange("p (h g k) -> p h g k", h=H, g=G)
            fh = first.rearrange("p (h r) k -> p h r k", h=H)
            for h in range(H):
                nc.vector.scalar_tensor_tensor(
                    out=tw[:, h], in0=fh[:, h, 0, :].rearrange("p (k o) -> p k o", o=1).broadcast_to([P, G, G]),
                    scalar=float(G) ** -0.5, in1=fh[:, h, 1:, :], op0=ALU.mult, op1=ALU.mult).then_inc(tw_ready, 1)

            def hidden(c):
                dve.wait_ge(gated, c + 1)
                nc.vector.tensor_tensor(hT[:, c, :], gate[c % 2], bank[2 + c % 4][:, N:2 * N], ALU.mult).then_inc(hid, 1)

            for c in range(HC):
                if c == 2:
                    dve.wait_ge(twT_ps, 1)
                    nc.vector.tensor_copy(twT[0:EX, :], bank[7][0:EX, 0:N]).then_inc(twT_ready, 1)
                hidden(c)
                for j in {5: (0,), 6: (1,), 7: (2, 3)}.get(c, ()):
                    dve.wait_ge(tw_ps, j + 1)
                    dve.wait_ge(hid, 2 * j + 2)
                    v = hT[:, 2 * j:2 * j + 2, :].rearrange("p c n -> p (c n)")
                    nc.vector.tensor_tensor(v, v, bank[(0, 1, 6, 7)[j]], ALU.mult).then_inc(hid_w, 1)
            for h in range(H):
                dve.wait_ge(down_ps, h + 1)
                nc.vector.tensor_tensor(xs[:, h, :], xs[:, h, :], bank[2 + h], ALU.add).then_inc(x2_ready, 1)
                dve.wait_ge(x2_ready, h + 1)
                variance(h)
                normalise(h)
                for k in range(2):
                    dve.wait_ge(part_a, 2 * h + k + 1)
                    dve.wait_ge(xn_ready, 2 * H + h + 1)
                    if k:
                        dve.wait_ge(part_r, 2 * h + 1)
                    nc.vector.tensor_tensor((xn, xparts[:, 2])[k][:, h, :], xn[:, h, :], xparts[:, k, h, :], ALU.subtract)\
                        .then_inc(part_r, 1)

            words = {}
            load_words(dve, words, 0)
            for t in range(1, BLOCKS[0], 2):
                dve.wait_ge(gat_ps, t + 1)
                nc.vector.tensor_copy(x1g[0][:, t, :], gather_bank(t)).then_inc(gathered_odd, 1)
            dve.wait_ge(gathered_odd, BLOCKS[0] // 2)
            for b in range(NB):
                tiles, p0 = BLOCKS[b], NP * b
                xg, es = x1g[b % 2], rest_sums[b]
                dve.wait_ge(gathered, copied_before(FIRST[b] + tiles))
                dve.wait_ge(edge_in[b], 16)
                dve.wait_ge(cleared, b + 1)

                def multiply(p):
                    i1, i2 = column(words, p0 + p, 0), column(words, p0 + p, 1)
                    if p0 + p >= SLOTS:
                        dve.wait_ge(psums, p0 + p + 1 - SLOTS)
                    nc.vector.scalar_tensor_tensor(
                        out=prod[:, (p0 + p) % SLOTS, 0:tiles], in0=xg[:, 0:tiles, bass.ds(i1, U)], scalar=coef_b[:, p:p + 1],
                        in1=edges[:, FIRST[b]:FIRST[b] + tiles, bass.ds(i2, U)],
                        op0=ALU.mult, op1=ALU.mult).then_inc(mults, 1)

                def add(p):
                    to = column(words, p0 + p, 2)
                    if p == 0:
                        dve.wait_ge(mults, p0 + p + 1)
                    if p0 + p:
                        dve.wait_ge(sums, p0 + p)
                    v = es[:, :, bass.ds(to, U)]
                    nc.vector.tensor_tensor(v, v, prod[:, (p0 + p) % SLOTS, KEPT[b]:tiles], ALU.add).then_inc(sums, 1)

                multiply(0)
                for p in range(NP):
                    if p + 1 < NP:
                        multiply(p + 1)
                    if p % PG == 4 and (b, p) < (NB - 1, NP - PG):
                        load_words(dve, words, p0 + (p // PG + 1) * PG)
                    add(p)
            for i in range(SPLIT + 1):
                if i < SPLIT:
                    v = tile_sums(NB - 1, split_tiles[i])
                    dve.wait_ge(hi_done, i + 1)
                    nc.vector.tensor_tensor(v, v, sum_parts[:, i, 0, :], ALU.subtract).then_inc(left_done, 1)
                if i:
                    dve.wait_ge(mid_done, i)
                    nc.vector.tensor_tensor(sum_parts[:, i - 1, 2, :], tile_sums(NB - 1, split_tiles[i - 1]),
                                            sum_parts[:, i - 1, 1, :], ALU.subtract).then_inc(lo_done, 1)
            for h in range(H):
                dve.wait_ge(half_done, h + 1)
                nc.vector.tensor_tensor(xs[:, h, :], xs[:, h, :], bank[2 + h], ALU.add).then_inc(x3_ready, 1)
                if h:
                    normalise(h - 1)
                dve.wait_ge(x3_ready, h + 1)
                variance(h)
            normalise(H - 1)
            copy_xnT(2, xnT2)
            dve.wait_ge(sel_ready, 4)
            dve.wait_ge(lg_ps, 1)
            link(nc.vector.scalar_tensor_tensor(out=logit[0:ES, :], in0=tie[0:ES, :], scalar=1e-6 / (TG - 1),
                                                in1=bank[4][0:ES, 0:N], op0=ALU.mult, op1=ALU.add))
            lg = logit[0:ES, :].rearrange("p (g t) -> p g t", t=TG)
            tp = top[0:ES, :].rearrange("p (g o) -> p g o", o=1)
            link(nc.vector.tensor_reduce(tp, lg, AX.X, ALU.max))
            link(nc.vector.tensor_tensor(permT[0:ES, :].rearrange("p (g t) -> p g t", t=TG), lg,
                                         tp.broadcast_to([ES, NG, TG]), ALU.is_equal))
            nc.vector.tensor_copy(permT_b[0:ES, :], permT[0:ES, :]).then_inc(perm_ready, 1)
            for h in range(H):
                dve.wait_ge(pt_ps, H)
                nc.vector.tensor_tensor(
                    perm_bd[:, h], bank[5][:, h * ES:(h + 1) * ES].rearrange("p (o e) -> p o e", o=1).broadcast_to([P, PH, ES]),
                    group_of.rearrange("p (g o) -> p g o", o=1).broadcast_to([P, PH, ES]), ALU.mult).then_inc(bd_ready, 1)
            for i in range(1, 2 * KC, 2):
                dve.wait_ge(y_ps, i + 1)
                nc.vector.tensor_copy(yT[:, i // 2, :, PH:].rearrange("p e g -> p g e"),
                                      bank[i % 4].rearrange("p (g e) -> p g e", e=ES)).then_inc(y_odd, 1)
            for k in range(2):
                dve.wait_ge(in_ps, k + 1)
                for q in range(2, EQ):
                    nc.vector.tensor_scalar(
                        inner[FE * q:FE * (q + 1), 8 * k:8 * k + 8, :],
                        bank[4 + k][FE * q:FE * (q + 1), :].rearrange("p (c e g) -> p c e g", e=EQ, g=NG)[:, :, q, :],
                        0.0, None, ALU.max).then_inc(in_high, 1)
                dve.wait_ge(in_low, 2 * (k + 1))
                dve.wait_ge(in_high, 2 * (k + 1))
                for j in range(k * FC // 4, (k + 1) * FC // 4):
                    dve.wait_ge(pf_ready, j + 1)
                    nc.vector.tensor_tensor(
                        z[:, 2 * j:2 * j + 2, :].rearrange("p c (g t) -> p (c g) t", t=TG),
                        perm_f[:, 2 * j:2 * j + 2, :].rearrange("p c (g t) -> p (c g) t", t=TG),
                        inner[:, 2 * j:2 * j + 2, :].rearrange("p c (g o) -> p (c g) o", o=1).broadcast_to([P, 2 * NG, TG]),
                        ALU.mult).then_inc(z_ready, 1)
            for h in range(H):
                dve.wait_ge(res_ps, h + 1)
                nc.vector.tensor_tensor(xs[:, h, :], xs[:, h, :], bank[6 + h], ALU.add).then_inc(fin, 1)

        @block.tensor
        def _(pe):
            mm = nc.tensor.matmul

            def keep_warm(to, n):
                for _ in range(n):
                    mm(to[:, 0:N], zero_b[:], iota_b[:], start=True, stop=True)

            def transpose_xn(stage):
                for h in range(H):
                    if stage:
                        keep_warm(bank[5], ((34, 6), (18, 12))[stage - 1][h])
                    pe.wait_ge(xn_ready, H * (stage if stage < 2 else 3) + h + 1)
                    for kc in range(KC):
                        last = nc.tensor.transpose(bank[kc // 2][:, (kc % 2) * N + h * P:(kc % 2) * N + (h + 1) * P],
                                                   xn[:, h, kc * P:(kc + 1) * P], ident[:])
                        if h == H - 1 and kc % 2 == 1:
                            last.then_inc(xnT_ps, 1)
                if stage:
                    keep_warm(bank[5], 8)
                pe.wait_ge(xnT_ready, 2 * (stage + 1))

            pe.wait_ge(const, 4 + 2 + H)
            pe.wait_ge(idx_ready, 2)
            def broadcast(q):
                if q >= 2:
                    pe.wait_ge(bc_copied, q - 1)
                for t in range(4 * q, min(4 * q + 4, T)):
                    last = mm(bank[6 + q % 2][:, (t % 4) * P:(t % 4 + 1) * P], src_b[:, t:t + 1].broadcast_to([P, P]),
                              ident_b, start=True, stop=True)
                last.then_inc(bc_ps, 1)

            def count(lo, hi):
                for t in range(lo, hi):
                    pe.wait_ge(onehot, 2 * (t + 1))
                    for h in range(H):
                        last = mm(bank[4 + h][:, 0:N], src_oh[:, t, h * P:(h + 1) * P], dst_ohb[:, t, :],
                                  start=t == 0, stop=t == T - 1)
                if hi == T:
                    last.then_inc(cnt_ps, 1)

            for q in range(QT):
                if q == 2:
                    keep_warm(bank[3], 16)
                broadcast(q)
                if 3 <= q < 7:
                    count(2 * (q - 3), 2 * (q - 2))
            transpose_xn(0)
            pe.wait_ge(w_in, 16)

            def project(h):
                for kc in range(KC):
                    last = mm(bank[2 + h], xnT[:, kc, h * P:(h + 1) * P], w_sb[:, kc, :], start=kc == 0, stop=kc == KC - 1)
                last.then_inc(h_ps, 1)

            def square(to, left, right, done, ready):
                for h in range(H):
                    for c in range(H):
                        pe.wait_ge(ready, c + 1)
                        last = mm(to[:, h * N:(h + 1) * N], left[:, c, h * P:(h + 1) * P], right[:, c, :],
                                  start=c == 0, stop=c == H - 1)
                last.then_inc(done, 1)

            count(T // 4, T // 2)
            project(0)
            count(T // 2, T)
            pe.wait_ge(link_ready, H)
            for h in range(H):
                for c in range(H):
                    o = bank[0][:, h * N + c * P:h * N + (c + 1) * P]
                    mm(o, ident_b, link_b[:, h, c * P:(c + 1) * P], start=True, stop=False)
                    last = mm(o, link_b[:, c, h * P:(h + 1) * P], ident_b, start=False, stop=True)
            last.then_inc(sym_ps, 1)
            project(1)
            square(bank[1], adj, cmat, s2_ps, cmat_ready)
            square(bank[4], cmat, series2, s3_ps, series2_ready)
            pe.wait_ge(h_ready, H)
            pe.wait_ge(bc_copied, QT)
            for h in range(H):
                for c in range(H):
                    pe.wait_ge(series_ready, c + 1)
                    last = mm(bank[6 + h], series[:, c, h * P:(h + 1) * P], cur[:, c, :], start=c == 0, stop=c == H - 1)
                last.then_inc(diff_ps, 1)

            transpose_xn(1)
            pe.wait_ge(small_in, 16 * 5)
            for h in range(H):
                for kc in range(KC):
                    last = mm(bank[6][:, h * (G + EX):(h + 1) * (G + EX)], xnT[:, kc, h * P:(h + 1) * P], w_cat[:, kc, :],
                              start=kc == 0, stop=kc == KC - 1)
            last.then_inc(logit_ps, 1)
            pe.wait_ge(w1_in, 16)
            pe.wait_ge(w3_in, 16)
            for c in range(HC):
                if c >= 4:
                    pe.wait_ge(hid, c - 3)
                for n, w in enumerate((w1_sb, w3_sb)):
                    for kc in range(KC):
                        last = mm(bank[2 + c % 4][:, n * N:(n + 1) * N], w[:, kc, c * P:(c + 1) * P], xnT[:, kc, :],
                                  start=kc == 0, stop=kc == KC - 1)
                last.then_inc(up_ps, 1)
                if c == 4:
                    pe.wait_ge(tw_ready, H)
                    for h in range(H):
                        last = nc.tensor.transpose(bank[7][0:EX, h * P:(h + 1) * P], tw_sb[:, h * EX:(h + 1) * EX], ident[:])
                    last.then_inc(twT_ps, 1)
                for j in {5: (0,), 6: (1, 2), 7: (3,)}.get(c, ()):
                    pe.wait_ge(twT_ready, 1)
                    pe.wait_ge(sel_ready, 1)
                    for i in (2 * j, 2 * j + 1):
                        last = mm(bank[(0, 1, 6, 7)[j]][:, (i % 2) * N:(i % 2 + 1) * N], spread[0:EX, i * P:(i + 1) * P],
                                  twT[0:EX, :], start=True, stop=True)
                    last.then_inc(tw_ps, 1)
            pe.wait_ge(w2_in, 16)
            for h in range(H):
                for c in range(HC):
                    if h == 0 and c % 2 == 0:
                        pe.wait_ge(hid_w, c // 2 + 1)
                    last = mm(bank[2 + h], hT[:, c, h * P:(h + 1) * P], w2_sb[:, c, :], start=c == 0, stop=c == HC - 1)
                last.then_inc(down_ps, 1)

            def gather_part(t, h, k):
                last = mm(gather_bank(t), src_t[:, h, t * P:(t + 1) * P], xparts[:, k, h, :],
                          start=h == 0 and k == 0, stop=h == H - 1 and k == 2)
                if h == H - 1 and k == 2:
                    last.then_inc(gat_ps, 1)

            def gather(t):
                if t >= BLOCKS[0] or t % 2 == 0:
                    pe.wait_ge(gathered, copied_before(t) if t >= BLOCKS[0] else copied_before(t - 7))
                else:
                    pe.wait_ge(gathered_odd, (t - 7) // 2)
                for h in range(H):
                    for k in range(3):
                        gather_part(t, h, k)

            def scatter(b, n, t):
                if t == FIRST[b]:
                    pe.wait_ge(block_out, banks_before(b + 1))
                pe.wait_ge(dst_made, n + 1)
                for h in range(H):
                    last = mm(bank[2 + h], dst_oh[:, n % DR, h * P:(h + 1) * P], tile_sums(b, t), start=n == 0, stop=False)
                last.then_inc(scattered, 1)

            def scatter_split(i):
                pe.wait_ge(dst_split_made, i + 1)
                pe.wait_ge(lo_done, i + 1)
                for h in range(H):
                    for k in range(3):
                        last = mm(bank[2 + h], dst_split[:, i, h * P:(h + 1) * P], sum_parts[:, i, k, :],
                                  start=False, stop=i == SPLIT - 1 and k == 2)
                    if i == SPLIT - 1:
                        last.then_inc(half_done, 1)

            pe.wait_ge(src_made, 2 * QT)
            pe.wait_ge(part_a, 2)
            pe.wait_ge(part_r, 2)
            pe.wait_ge(x2_ready, 1)
            for t in range(8):
                if t == 7:
                    pe.wait_ge(x2_ready, H)
                for k in range(3):
                    gather_part(t, 0, k)
            for k in range(3):
                pe.wait_ge((part_a, part_a, part_r)[k], (3, 4, 4)[k])
                for t in range(8):
                    gather_part(t, 1, k)
            for t in range(8, BLOCKS[0]):
                gather(t)
            pe.wait_ge(packed, 1)
            words = {}
            load_words(pe, words, 0)
            for b in range(NB):
                gathers = list(range(FIRST[b + 1], FIRST[b + 1] + BLOCKS[b + 1])) if b + 1 < NB else []
                scatters = scatter_order(b - 1) if b else []
                scatter_at = [1 + i * (NP - 4) // len(scatters) for i in range(len(scatters))]
                gather_at = [3 + i * (NP - 4) // len(gathers) for i in range(len(gathers))]
                if b:
                    pe.wait_ge(block_out, banks_before(b))
                    pe.wait_ge(sums, NP * b)
                else:
                    pe.wait_ge(gathered, copied_before(BLOCKS[0]))
                    pe.wait_ge(gathered_odd, BLOCKS[0] // 2)
                for q in sum_banks(b):
                    mm(bank[q], zero_b[:], src_t[:, 0, 0:512], start=True, stop=False)
                for p in range(NP):
                    to = column(words, NP * b + p, 2)
                    pe.wait_ge(mults, NP * b + p + 1)
                    slot = (NP * b + p) % SLOTS
                    last = mm(path_sums(to), ident[:], prod[:, slot, 0:PT].rearrange("p t u -> p (t u)"),
                              start=False, stop=False, skip_group_check=True)
                    if KEPT[b] > PT:
                        last = mm(psum[:, bass.ds(to + 512, U)], ident[:], prod[:, slot, PT, :],
                                  start=False, stop=False, skip_group_check=True)
                    last.then_inc(psums, 1)
                    if p in scatter_at:
                        scatter(b - 1, *scatters[scatter_at.index(p)])
                    if p in gather_at:
                        gather(gathers[gather_at.index(p)])
                    if p % PG == 7 and (b, p) < (NB - 1, NP - PG):
                        load_words(pe, words, NP * b + (p // PG + 1) * PG)
                for q in sum_banks(b):
                    mm(bank[q], zero_b[:], src_t[:, 0, 0:512], start=False, stop=True).then_inc(block_ps, 1)
            pe.wait_ge(sums, NP * NB)
            for n, t in scatter_order(NB - 1)[:BLOCKS[NB - 1] - SPLIT]:
                scatter(NB - 1, n, t)
            for i in range(SPLIT):
                scatter_split(i)

            transpose_xn(2)
            pe.wait_ge(ctrl_in, 16)
            for kc in range(KC):
                last = mm(bank[4][0:ES, 0:N], ctrl_sb[:, kc, :], xnT2[:, kc, :], start=kc == 0, stop=kc == KC - 1)
            last.then_inc(lg_ps, 1)
            keep_warm(bank[7], 18)
            pe.wait_ge(perm_ready, 1)
            for h in range(H):
                nc.tensor.transpose(bank[5][:, h * ES:(h + 1) * ES], permT[0:ES, h * P:(h + 1) * P], ident[0:ES, 0:ES])\
                    .then_inc(pt_ps, 1)

            def spread_perm(lo, hi):
                for j in range(lo, hi):
                    if j in (2, 3):
                        pe.wait_ge(pf_ready, j - 1)
                    for c in (2 * j, 2 * j + 1):
                        last = mm(perm_bank(j)[:, (c % 2) * N:(c % 2 + 1) * N], select[0:ES, c * P:(c + 1) * P],
                                  permT_b[0:ES, :], start=True, stop=True)
                    last.then_inc(pf_ps, 1)

            spread_perm(0, 2)
            keep_warm(bank[3], 4)
            pe.wait_ge(bd_ready, H)
            for i in range(2 * KC):
                if i >= 4:
                    pe.wait_ge((y_even, y_odd)[i % 2], (i - 4) // 2 + 1)
                mm(bank[i % 4], xn[:, i % 2, (i // 2) * P:(i // 2 + 1) * P], perm_bd[:, i % 2].rearrange("p g e -> p (g e)"),
                   start=True, stop=True).then_inc(y_ps, 1)
            spread_perm(2, 4)
            pe.wait_ge(y_even, KC)
            pe.wait_ge(y_odd, KC)
            pe.wait_ge(f1_in, 16)
            for c in range(FC):
                for kc in range(KC):
                    last = mm(bank[4 + c // 8][:, (c % 8) * EQ * NG:(c % 8 + 1) * EQ * NG], f1_sb[:, kc, c * P:(c + 1) * P],
                              yT[:, kc, c * EQ:(c + 1) * EQ, :].rearrange("p e g -> p (e g)"), start=kc == 0, stop=kc == KC - 1)
                if c % 8 == 7:
                    last.then_inc(in_ps, 1)
                if c == 7:
                    spread_perm(4, FC // 2)
            pe.wait_ge(pf_ready, FC // 2)
            pe.wait_ge(f2_in, 16)
            pe.wait_ge(f2b_in, 16)
            for h in range(H):
                for c in range(FC):
                    if h == 0 and c % 2 == 0:
                        pe.wait_ge(z_ready, c // 2 + 1)
                    last = mm(bank[6 + h], z[:, c, h * P:(h + 1) * P], f2_sb(c), start=c == 0, stop=c == FC - 1)
                last.then_inc(res_ps, 1)


def kernel(**inputs):
    import numpy as np
    import concourse.bacc as bacc
    from concourse.bass_utils import run_bass_kernel_spmd

    a = {k: np.asarray(v) for k, v in inputs.items()}
    E, D, HID = a["L0_ffn_W1"].shape
    arrays = {
        "x": a["x"], "src": a["src"], "dst": a["dst"], "edge": a["edge_attr_512"],
        "gnn_w": a["L0_gnn_W"], "gnn_b": a["L0_gnn_b"], "diff_w": a["L0_gnn_diffusion_weights"],
        "wr": a["L0_ffn_Wr"], "br": a["L0_ffn_br"],
        "wgate": a["L0_ffn_Wgate"].transpose(1, 0, 2).reshape(D, -1), "bgate": a["L0_ffn_bgate"].reshape(-1),
        "w1": a["L0_ffn_W1"].transpose(1, 0, 2).reshape(D, -1), "w3": a["L0_ffn_W3"].transpose(1, 0, 2).reshape(D, -1),
        "w2": a["L0_ffn_W2"].reshape(-1, D), "coef": a["L1_gnn_path_coeffs"], "paths": a["L1_gnn_path_indices"],
        "ctrl": a["L1_ffn_controller"].reshape(D, -1), "f1": a["L1_ffn_f1"].reshape(D, -1), "f2": a["L1_ffn_f2"].reshape(-1, D),
    }
    arrays = {k: np.ascontiguousarray(v) for k, v in arrays.items()}
    nc = bacc.Bacc("TRN2", target_bir_lowering=False, num_devices=1)
    args = [nc.dram_tensor(f"in_{k}", v.shape, mybir.dt.from_np(v.dtype), kind="ExternalInput").ap()
            for k, v in arrays.items()]
    out = nc.dram_tensor("out", a["x"].shape, mybir.dt.float32, kind="ExternalOutput").ap()
    graph_and_experts(nc, *args, out)
    r = run_bass_kernel_spmd(nc, [{f"in_{k}": v for k, v in arrays.items()}], core_ids=[0])
    return r.results[0]["out"]
```
